# Optimizing a Trainium2 kernel written in Bass

```python
import numpy as np
import jax
import jax.numpy as jnp

def _softmax(x, axis=-1):
    return jax.nn.softmax(x, axis=axis)
def _gelu(x):
    return jax.nn.gelu(x, approximate=True)
def _silu(x):
    return jax.nn.silu(x)
def _sigmoid(x):
    return jax.nn.sigmoid(x)
def _layernorm(x, axis=-1, eps=1e-5):
    m = jnp.mean(x, axis=axis, keepdims=True)
    v = jnp.var(x, axis=axis, keepdims=True)
    return (x - m) / jnp.sqrt(v + eps)
def _scatter_add(tgt, idx, src, axis=0):
    return tgt.at[idx].add(src)
def _segment_sum(src, seg, n):
    return jax.ops.segment_sum(src, seg, n)

kernel_name = 'mk_adj_preln_d1_adj_1024_094b8a'

def setup_inputs(seed: int = 0):
    np.random.seed(seed)
    _w = jnp.asarray
    def _rec_inputs():
        import jax
        import jax.numpy as jnp
        _gk = jax.random.key(seed)
        x = -0.0002928 + 1 * jax.random.normal(jax.random.fold_in(_gk, 1), (4096, 1024), jnp.float32)
        _a = jax.random.bernoulli(jax.random.fold_in(_gk, 2), 0.00390625, (4096, 4096))
        _a = jnp.logical_or(_a, jnp.swapaxes(_a, -1, -2))
        _a = jnp.logical_or(_a, jnp.eye(4096, dtype=bool))
        _af = _a.astype(jnp.float32)
        adj = _af
        return x, adj
    x, adj = _rec_inputs()
    def _L0_gnn_setup():
        import jax, jax.numpy as jnp
        import numpy as np
        N = 4096
        D_IN = 1024
        H = 16
        DH = D_IN // H
        ALPHA = 0.2
        MASK_VAL = -65500.0
        key = jax.random.key(seed)
        ks = jax.random.split(key, 7)
        x = jax.random.normal(ks[0], (N, D_IN), dtype=jnp.float32)
        adj = jax.random.randint(ks[1], (N, N), 0, 2).astype(jnp.float32)
        s = 1.0 / np.sqrt(D_IN)
        W_seq = jax.random.normal(ks[2], (D_IN, D_IN), dtype=jnp.float32) * s
        a1 = jax.random.normal(ks[3], (DH,), dtype=jnp.float32) / np.sqrt(DH)
        a2 = jax.random.normal(ks[4], (DH,), dtype=jnp.float32) / np.sqrt(DH)
        W_out = jax.random.normal(ks[5], (D_IN, D_IN), dtype=jnp.float32) * s
        b_out = jax.random.normal(ks[6], (D_IN,), dtype=jnp.float32) * 0.01
        return {'x': x, 'adj': adj, 'W_seq': W_seq, 'a1': a1, 'a2': a2, 'W_out': W_out, 'b_out': b_out}
    _L0_gnn_all = _L0_gnn_setup()
    _L0_gnn_in = {k: v for k, v in _L0_gnn_all.items() if k in ('W_seq', 'a1', 'a2', 'W_out', 'b_out', )}
    del _L0_gnn_all

    return {
        "x": x,
        "adj": adj,
        "L0_gnn_W_seq": _L0_gnn_in["W_seq"],
        "L0_gnn_a1": _L0_gnn_in["a1"],
        "L0_gnn_a2": _L0_gnn_in["a2"],
        "L0_gnn_W_out": _L0_gnn_in["W_out"],
        "L0_gnn_b_out": _L0_gnn_in["b_out"],
    }

def reference(x, adj, L0_gnn_W_seq, L0_gnn_a1, L0_gnn_a2, L0_gnn_W_out, L0_gnn_b_out):
    import jax
    import jax.numpy as jnp
    def _L0_gnn_ref(x, adj, W_seq, a1, a2, W_out, b_out):
        import jax, jax.numpy as jnp
        import numpy as np
        N = 4096
        D_IN = 1024
        H = 16
        DH = D_IN // H
        ALPHA = 0.2
        MASK_VAL = -65500.0
        seq = (x @ W_seq).reshape(N, H, DH)
        score1 = jnp.einsum('nhd,d->hn', seq, a1)
        score2 = jnp.einsum('nhd,d->hn', seq, a2)
        scores = score1[:, :, None] + score2[:, None, :]
        scores = jax.nn.leaky_relu(scores, negative_slope=ALPHA)
        scores = scores + (1.0 - adj)[None, :, :] * MASK_VAL
        attn = jax.nn.softmax(scores, axis=-1)
        hidden = jnp.einsum('hij,jhd->ihd', attn, seq).reshape(N, D_IN)
        hidden = hidden @ W_out + b_out
        return jax.nn.elu(hidden)

    h = jnp.maximum(_layernorm(x, axis=-1), 0.0)
    x = x + _L0_gnn_ref(h, adj, L0_gnn_W_seq, L0_gnn_a1, L0_gnn_a2, L0_gnn_W_out, L0_gnn_b_out)
    return x


_drawn_inputs = setup_inputs


def setup_inputs(seed=0):
    import zlib

    import numpy as np

    out = dict(_drawn_inputs(seed))
    spreads = {}
    factors = {'L0_gnn_a1': 3.409, 'L0_gnn_b_out': 6.555}
    for name, (base, spread) in spreads.items():
        noise = np.random.default_rng([zlib.crc32(name.encode()), seed]).standard_normal(out[name].shape)
        drawn = base * np.exp(spread * noise) if base else spread * noise
        out[name] = jnp.asarray(drawn.astype(out[name].dtype))
    for name, factor in factors.items():
        out[name] = (out[name] * factor).astype(out[name].dtype)
    return out
```

```python
from contextlib import ExitStack

import concourse.bass as bass
from concourse import mybir

F32 = mybir.dt.float32
F16 = mybir.dt.float16
BF16 = mybir.dt.bfloat16
F8 = mybir.dt.float8e4
U8 = mybir.dt.uint8
I8 = mybir.dt.int8
U32 = mybir.dt.uint32
ALU = mybir.AluOpType
ACT = mybir.ActivationFunctionType
AX_X = mybir.AxisListType.X
RMAX = bass.bass_isa.ReduceOp.max

P = 128
ALPHA = 0.2
EPS = 1e-5
ONE_F8 = 0x38
LO_SCALE = 4096.0
E_SCALE = 64.0


def build(nc, x, adj, w_seq, a1, a2, w_out, b_out, out):
    N, D = x.shape
    DH = a1.shape[0]
    H = D // DH
    T = N // P
    K = D // P
    BANK = 512
    NY = D // BANK
    Q = 4
    QJ = T // Q

    IG = 8
    GI = IG * P
    NG = T // IG
    J = 4
    C = T // J
    M1_SLOTS, M0_SLOTS = 4, 2
    DC = DH + 1
    NV = 4 * DC
    QT = T // NG
    PK = 5 * T
    ON_DVE = (0, 3, 4, 5, 6, 7)
    assert T % IG == 0 and QT * NG == T and NV <= BANK

    seq_d = nc.dram_tensor("seq_by_head", (H, P, T, DH), F32, kind="Internal").ap()
    pack_d = nc.dram_tensor("pack_by_head", (H, P, PK), F32, kind="Internal").ap()
    arow_d = nc.dram_tensor("a_by_head", (H, N), F32, kind="Internal").ap()
    hid_d = nc.dram_tensor("hidden", (N, D), F32, kind="Internal").ap()

    def tools(ctx):
        return (lambda name, shape, dt: ctx.enter_context(nc.sbuf_tensor(name, shape, dt)),
                lambda name, shape, dt: ctx.enter_context(nc.psum_tensor(name, shape, dt)),
                lambda name: ctx.enter_context(nc.semaphore(name)))

    def identity(pool, tile, zeroed, made):
        pool.memset(tile[:], 0.0).then_inc(zeroed, 1)
        pool.wait_ge(zeroed, 1)
        pool.affine_select(out=tile[:], in_=tile[:], compare_op=ALU.not_equal, fill=1.0, base=0,
                           pattern=[[-1, P]], channel_multiplier=1).then_inc(made, 1)

    def project(adjT, A, B):
        with ExitStack() as ctx:
            sb, ps, sem = tools(ctx)
            w = sb("w_seq_sb", [P, K, D], F32)
            x_in = sb("x_in", [P, D], F32)
            xn = sb("xn", [P, D], F32)
            hT = sb("hT", [P, 2, K, P], F32)
            seq = sb("seq", [P, H, DH], F32)
            prod = sb("prod", [P, H, DH], F32)
            adj_in = sb("adj_in", [P, Q, QJ * P], F32)
            ident = sb("ident", [P, P], F32)
            ident16 = sb("ident16", [P, P], BF16)
            a12 = sb("a12", [P, 2, DH], F32)
            stats = sb("stats", [P, 2, 6], F32)
            mv = sb("mv", [P, 2], F32)
            var = sb("var", [P, 1], F32)
            std = sb("std", [P, 1], F32)
            rstd = sb("rstd", [P, 1], F32)
            xT_ps = ps("xT_ps", [P, K, P], F32)
            y_ps = ps("y_ps", [P, 2, D], F32)
            adj_ps = ps("adj_ps", [P, 2, QJ, P], BF16)

            w_loaded = sem("w_loaded")
            a12_loaded = sem("a12_loaded")
            x_loaded = sem("x_loaded")
            adj_loaded = [sem(f"adj_loaded{q}") for q in range(Q)]
            adj_turned = sem("adj_turned")
            adj_bank_free = sem("adj_bank_free")
            zeroed, zeroed16 = sem("zeroed"), sem("zeroed16")
            ident_made = sem("ident_made")
            stats_made = sem("stats_made")
            stats_seen = sem("stats_seen")
            mv_made = sem("mv_made")
            var_made = sem("var_made")
            std_made = sem("std_made")
            rstd_made = sem("rstd_made")
            xn_made = sem("xn_made")
            xT_done = sem("xT_done")
            hT_made = sem("hT_made")
            y_done = sem("y_done")
            seq_made = sem("seq_made")
            seq_stored = sem("seq_stored")
            prod_made = sem("prod_made")
            score_made = sem("score_made")
            block = ctx.enter_context(nc.Block())

            @block.sync
            def _(sp):
                sp.dma_start(x_in[:], x[0:P, :]).then_inc(x_loaded, 16)
                sp.dma_start(w[:], w_seq.rearrange("(k p) n -> p k n", p=P)).then_inc(w_loaded, 16)
                sp.dma_start(a12[:, 0, :], a1.partition_broadcast(P)).then_inc(a12_loaded, 16)
                sp.dma_start(a12[:, 1, :], a2.partition_broadcast(P)).then_inc(a12_loaded, 16)
                with sp.Fori(0, T) as t:
                    for q in range(Q):
                        sp.wait_ge(adj_turned, Q * t + q + 1)
                        sp.dma_start(adj_in[:, q, :], adj[bass.ts(t, P), q * QJ * P:(q + 1) * QJ * P]
                                     ).then_inc(adj_loaded[q], 16)
                        if q == 1:
                            sp.wait_ge(xn_made, t + 2)
                            sp.dma_start(x_in[:], x[bass.ts((t + 1) % T, P), :]).then_inc(x_loaded, 16)

            @block.gpsimd
            def _(pool):
                identity(pool, ident, zeroed, ident_made)
                identity(pool, ident16, zeroed16, ident_made)

            @block.vector
            def _(dve):
                def norm(t):
                    dve.wait_ge(x_loaded, 16 * (t + 1))
                    for n in range(2):
                        dve.bn_stats(stats[:, n, :], x_in[:, n * D // 2:(n + 1) * D // 2]).then_inc(stats_made, 1)
                    dve.wait_ge(stats_made, 2 * (t + 1))
                    dve.sem_inc(stats_seen, 1)
                    dve.wait_ge(xn_made, t + 1)
                    dve.sem_inc(stats_seen, 1)
                    dve.bn_aggr(mv[:], stats[:]).then_inc(mv_made, 1)
                    dve.wait_ge(mv_made, t + 1)
                    dve.tensor_scalar(var[:], mv[:, 1:2], EPS, None, ALU.add).then_inc(var_made, 1)
                    dve.wait_ge(std_made, t + 1)
                    dve.reciprocal(rstd[:], std[:]).then_inc(rstd_made, 1)
                    dve.wait_ge(rstd_made, t + 1)
                    dve.wait_ge(xT_done, 2 * t + 1)
                    dve.tensor_scalar(xn[:], x_in[:], mv[:, 0:1], rstd[:], ALU.subtract, ALU.mult
                                      ).then_inc(xn_made, 1)

                dve.sem_inc(seq_made, 2)
                dve.sem_inc(xn_made, 1)
                dve.sem_inc(score_made, 1)
                norm(0)
                dve.wait_ge(a12_loaded, 32)
                with dve.Fori(0, T // 2) as tp:
                    for s in range(2):
                        t = 2 * tp + s
                        norm(t + 1)
                        dve.wait_ge(y_done, t + 3)
                        dve.wait_ge(seq_stored, 16 * (t + 1))
                        dve.tensor_copy(seq[:].rearrange("p h d -> p (h d)"), y_ps[:, s, :]).then_inc(seq_made, 1)
                        dve.wait_ge(seq_made, t + 3)
                        for n, S in enumerate((A, B)):
                            dve.wait_ge(score_made, 2 * t + n + 1)
                            dve.tensor_tensor(prod[:], seq[:],
                                              a12[:, n:n + 1, :].to_broadcast([P, H, DH]), ALU.mult
                                              ).then_inc(prod_made, 1)
                            dve.wait_ge(prod_made, 2 * t + n + 1)
                            dve.tensor_reduce(S[:, bass.ds(t, 1), :], prod[:], AX_X, ALU.add
                                              ).then_inc(score_made, 1)

            @block.scalar
            def _(act):
                def root(t):
                    act.wait_ge(var_made, t + 1)
                    act.activation(std[:], var[:], ACT.Sqrt).then_inc(std_made, 1)

                def take_h(t, s):
                    act.wait_ge(y_done, t + 1)
                    for n in range(2):
                        act.wait_ge(xT_done, 2 * t + n + 2)
                        act.activation(hT[:, s, n * K // 2:(n + 1) * K // 2, :],
                                       xT_ps[:, n * K // 2:(n + 1) * K // 2, :], ACT.Relu
                                       ).then_inc(hT_made, 1)

                def take_adj(t, q):
                    act.wait_ge(adj_turned, Q * (t + 1) + q + 1)
                    act.activation(adjT[:, q * QJ:(q + 1) * QJ, bass.ts(t, P)], adj_ps[:, q % 2, :, :],
                                   ACT.Copy, scale=float(ONE_F8)).then_inc(adj_bank_free, 1)

                act.sem_inc(adj_bank_free, 2)
                act.sem_inc(hT_made, 2)
                act.sem_inc(seq_stored, 16)
                root(0)
                take_h(0, 0)
                with act.Fori(0, T // 2) as tp:
                    for s in range(2):
                        t = 2 * tp + s
                        root(t + 1)
                        take_adj(t, 0)
                        take_adj(t, 1)
                        take_h(t + 1, 1 - s)
                        take_adj(t, 2)
                        take_adj(t, 3)
                        act.wait_ge(seq_made, t + 3)
                        act.dma_start(seq_d[:, :, bass.ds(t, 1), :].rearrange("h p t d -> p h (t d)"), seq[:]
                                      ).then_inc(seq_stored, 16)
                act.wait_ge(seq_stored, 16 * (T + 1))

            @block.tensor
            def _(pe):
                def turn_x(t):
                    pe.wait_ge(xn_made, t + 2)
                    pe.wait_ge(hT_made, 2 * t + 2)
                    for k in range(K):
                        i = pe.transpose(xT_ps[:, k, :], xn[:, k * P:(k + 1) * P], ident[:])
                        if k % (K // 2) == K // 2 - 1:
                            i.then_inc(xT_done, 1)

                def turn_adj(t, q):
                    pe.wait_ge(adj_loaded[q], 16 * (t + 1))
                    pe.wait_ge(adj_bank_free, Q * t + q + 1)
                    upper = adj_in[:, q, :].bitcast(BF16).rearrange("p (j c two) -> p j c two", j=QJ, two=2)
                    for j in range(QJ):
                        i = pe.transpose(adj_ps[:, q % 2, j, :], upper[:, j, :, 1], ident16[:])
                    i.then_inc(adj_turned, 1)

                pe.sem_inc(y_done, 2)
                pe.sem_inc(adj_turned, Q)
                pe.sem_inc(xT_done, 1)
                pe.wait_ge(ident_made, 2)
                turn_x(0)
                pe.wait_ge(w_loaded, 16)
                with pe.Fori(0, T // 2) as tp:
                    for s in range(2):
                        t = 2 * tp + s
                        turn_adj(t, 0)
                        turn_adj(t, 1)
                        pe.wait_ge(seq_made, t + 1)
                        for k in range(K):
                            if k % (K // 2) == 0:
                                pe.wait_ge(hT_made, 2 * t + 2 * k // K + 3)
                            if k == K // 2:
                                turn_x(t + 1)
                            for n in range(NY):
                                i = pe.matmul(y_ps[:, s, n * BANK:(n + 1) * BANK], hT[:, s, k, :],
                                              w[:, k, n * BANK:(n + 1) * BANK], start=k == 0, stop=k == K - 1)
                        i.then_inc(y_done, 1)
                        turn_adj(t, 2)
                        turn_adj(t, 3)

    def factors(A, B):
        with ExitStack() as ctx:
            sb, ps, sem = tools(ctx)
            ident = sb("ident_f", [P, P], F32)
            top = sb("top", [P, H], F32)
            bmax = sb("bmax", [P, H], F32)
            diff = sb("diff", [P, H, T], F32)
            z = sb("z", [P, H, T], F32)
            zlo = sb("zlo", [P, H, T], F32)
            zhi = sb("zhi", [P, H, T], F32)
            e = sb("e", [P, 2, H, T], F32)
            pack = sb("pack", [P, H, PK], F32)
            aT = sb("aT", [H, N], F32)
            aT_ps = ps("aT_ps", [P, 2, BANK], F32)
            zeroed, ident_made = sem("zeroed_f"), sem("ident_made_f")
            top_made, bmax_made = sem("top_made"), sem("bmax_made")
            args_made = sem("args_made")
            e_made, pack_made = sem("e_made"), sem("pack_made")
            aT_done, aT_taken = sem("aT_done"), sem("aT_taken")
            stored = sem("factors_stored")
            block = ctx.enter_context(nc.Block())

            @block.gpsimd
            def _(pool):
                identity(pool, ident, zeroed, ident_made)
                pool.wait_ge(top_made, 1)
                pool.partition_all_reduce(bmax[:], top[:], P, RMAX).then_inc(bmax_made, 1)

            @block.vector
            def _(dve):
                def heads_first(S):
                    return S[:].rearrange("p t h -> p h t")

                dve.tensor_reduce(top[:], heads_first(B), AX_X, ALU.max).then_inc(top_made, 1)
                dve.tensor_scalar(pack[:, :, 0:T], heads_first(B), -1.0, None, ALU.mult).then_inc(pack_made, 1)
                dve.wait_ge(bmax_made, 1)
                wide = bmax[:].unsqueeze(2).to_broadcast([P, H, T])
                dve.tensor_tensor(diff[:], heads_first(B), wide, ALU.subtract).then_inc(args_made, 1)
                dve.tensor_tensor(z[:], heads_first(A), wide, ALU.add).then_inc(args_made, 1)
                dve.wait_ge(args_made, 2)
                dve.tensor_scalar(zlo[:], z[:], 0.0, 1.0 - ALPHA, ALU.min, ALU.mult).then_inc(args_made, 1)
                dve.tensor_scalar(zhi[:], z[:], 0.0, ALPHA - 1.0, ALU.max, ALU.mult).then_inc(args_made, 1)
                dve.wait_ge(e_made, 2)
                for n in range(2):
                    dve.tensor_scalar(pack[:, :, (n + 1) * T:(n + 2) * T], e[:, n, :, :], E_SCALE * LO_SCALE,
                                      None, ALU.mult).then_inc(pack_made, 1)

            @block.tensor
            def _(pe):
                pe.wait_ge(ident_made, 1)
                for g in range(T // 4):
                    if g >= 2:
                        pe.wait_ge(aT_taken, g - 1)
                    for n in range(4):
                        i = pe.transpose(aT_ps[0:H, g % 2, n * P:(n + 1) * P], A[:, 4 * g + n, :], ident[:])
                    i.then_inc(aT_done, 1)

            @block.scalar
            def _(act):
                for g in range(T // 4):
                    act.wait_ge(aT_done, g + 1)
                    act.activation(aT[:, g * BANK:(g + 1) * BANK], aT_ps[0:H, g % 2, :], ACT.Copy
                                   ).then_inc(aT_taken, 1)
                act.wait_ge(args_made, 4)
                act.activation(e[:, 0], diff[:], ACT.Exp).then_inc(e_made, 1)
                act.activation(e[:, 1], diff[:], ACT.Exp, scale=ALPHA).then_inc(e_made, 1)
                F = pack[:, :, 3 * T:5 * T].rearrange("p h (t two) -> p h t two", two=2)
                act.activation(F[:, :, :, 0], zlo[:], ACT.Exp).then_inc(pack_made, 1)
                act.activation(F[:, :, :, 1], zhi[:], ACT.Exp).then_inc(pack_made, 1)

            @block.sync
            def _(sp):
                sp.wait_ge(aT_taken, T // 4)
                sp.dma_start(arow_d, aT[:]).then_inc(stored, 16)
                sp.wait_ge(pack_made, 5)
                sp.dma_start(pack_d.rearrange("h p c -> p h c"), pack[:]).then_inc(stored, 16)
                sp.wait_ge(stored, 32)

    def attend(adjT):
        with ExitStack() as ctx:
            sb, ps, sem = tools(ctx)
            arow = sb("arow", [P, 2, GI], F32)
            m1 = sb("m1", [P, M1_SLOTS, J, GI], F8)
            m0 = sb("m0", [P, M0_SLOTS, J, GI], F8)
            vals = sb("vals", [P, 2, T, 2, 2, DC], F16)
            pack = sb("pack_h", [P, 2, PK], F32)
            seq1 = sb("seq1", [P, QT, DC], F32)
            prod = sb("prod_v", [P, 2, QT, DC], F32)
            lo_part = sb("lo_part", [P, 2, 2, 2, DC], F32)
            side = sb("side", [P, IG, 2, DC], F32)
            both, hid = side[:, :, 0, :], side[:, :, 1, 0:DH]
            rden = sb("rden", [P, IG, 1], F32)
            acc = ps("acc", [P, IG, BANK], F32)

            pack_loaded = [sem(f"pack_loaded{n}") for n in range(2)]
            seq_loaded = sem("seq_loaded")
            arow_loaded = [sem(f"arow_loaded{n}") for n in range(2)]
            ones_made = sem("ones_made")
            prod_made = sem("prod_v_made")
            hi_made = sem("hi_made")
            vals_made = sem("vals_made")
            above_act = sem("above_act")
            above_dve = sem("above_dve")
            m1_made = sem("m1_made")
            m0_made = sem("m0_made")
            masks_used = sem("masks_used")
            waits_passed = sem("waits_passed")
            acc_done = sem("acc_done")
            lo_taken = sem("lo_taken")
            acc_free = sem("acc_free")
            sides_scaled = sem("sides_scaled")
            both_made = sem("both_made")
            rden_made = sem("rden_made")
            hid_made = sem("hid_made")
            hid_stored = sem("hid_stored")
            block = ctx.enter_context(nc.Block())

            def head(hp, s, ahead):
                return (2 * hp + s + ahead) % H

            @block.sync
            def _(sp):
                def load_seq(h, q):
                    sp.dma_start(seq1[:, :, 0:DH], seq_d[bass.ds(h, 1), :, q * QT:(q + 1) * QT, :]
                                 .rearrange("h p t d -> (h p) t d")).then_inc(seq_loaded, 16)

                def load_pack(h, slot):
                    sp.dma_start(pack[:, slot, :], pack_d[bass.ds(h, 1), :, :].rearrange("h p c -> (h p) c")
                                 ).then_inc(pack_loaded[slot], 16)

                def load_arow(h, g, slot):
                    sp.dma_start(arow[:, slot, :], arow_d[bass.ds(h, 1), g * GI:(g + 1) * GI]
                                 .rearrange("h n -> (h n)").partition_broadcast(P)).then_inc(arow_loaded[slot], 16)

                sp.sem_inc(hid_stored, 16)
                load_pack(0, 0)
                load_arow(0, 0, 0)
                for q in range(NG):
                    if q:
                        sp.wait_ge(prod_made, 2 * q)
                    load_seq(0, q)
                with sp.Fori(0, H // 2) as hp:
                    for s in range(2):
                        for g in range(NG):
                            n = (2 * hp + s) * NG + g
                            if g == 0:
                                sp.wait_ge(hid_made, n + 1)
                                load_pack(head(hp, s, 1), 1 - s)
                            sp.wait_ge(m1_made, C * n + 1)
                            load_arow(head(hp, s, (g + 1) // NG), (g + 1) % NG, (g + 1) % 2)
                            sp.wait_ge(prod_made, 2 * (n + NG))
                            load_seq(head(hp, s, 1), g)
                            sp.wait_ge(hid_made, n + 2)
                            sp.dma_start(hid_d[g * GI:(g + 1) * GI, :]
                                         .rearrange("(t p) c -> p t c", p=P)[:, :, bass.ts(2 * hp + s, DH)],
                                         hid).then_inc(hid_stored, 16)
                sp.wait_ge(hid_stored, 16 * (H * NG + 1))
                for slot in range(2):
                    sp.wait_ge(pack_loaded[slot], 16 * (H // 2 + 1 - slot))
                    sp.wait_ge(arow_loaded[slot], 16 * (H * NG // 2 + 1 - slot))

            @block.scalar
            def _(act):
                def compare(hp, s, g, c):
                    hs, gs = (s + (g // NG)) % 2, g % NG
                    grp = (2 * hp + s) * NG + g
                    n = grp * C + c
                    act.wait_ge(masks_used, n + 1)
                    if c == 0:
                        act.wait_ge(arow_loaded[gs % 2], 16 * ((2 * hp + s) * (NG // 2) + g // 2 + 1))
                    for j in range(J - (c in ON_DVE)):
                        i = act.activation(m1[:, c % M1_SLOTS, j, :].bitcast(I8), arow[:, gs % 2, :], ACT.Sign,
                                           bias=pack[:, hs, c * J + j:c * J + j + 1], scale=-1.0)
                    i.then_inc(above_act, 1)

                def hi(q, slot, qq, e):
                    act.wait_ge(prod_made, 2 * q + e + 1)
                    act.activation(vals[:, slot, qq * QT:(qq + 1) * QT, e, 0, :], prod[:, e, :, :], ACT.Copy,
                                   scale=1.0 / LO_SCALE).then_inc(hi_made, 1)

                act.wait_ge(pack_loaded[0], 16)
                act.sem_inc(acc_free, 4)
                for q in range(NG):
                    for e in range(2):
                        hi(q, 0, q, e)
                for c in range(C // 2):
                    compare(0, 0, 0, c)
                with act.Fori(0, H // 2) as hp:
                    for s in range(2):
                        for g in range(NG):
                            n = (2 * hp + s) * NG + g
                            for c in range(C // 2, C):
                                compare(hp, s, g, c)
                                if c in (C // 2 + 1, C // 2 + 2):
                                    if g == 0 and c == C // 2 + 1:
                                        act.wait_ge(masks_used, M1_SLOTS + C * n)
                                    hi(n + NG, 1 - s, g, c - C // 2 - 1)
                            if g == NG - 1:
                                act.wait_ge(pack_loaded[1 - s], 16 * (hp + 1 + s))
                            compare(hp, s, g + 1, 0)
                            compare(hp, s, g + 1, 1)
                            for p in range(IG // 2):
                                if p < IG // 2 - 1:
                                    act.wait_ge(acc_done, 3 * n + p + 1)
                                else:
                                    act.wait_ge(masks_used, M1_SLOTS + C * (n + 1))
                                act.wait_ge(acc_free, 4 * n + p + 3)
                                acc4 = acc[:, 2 * p:2 * p + 2, 0:NV].rearrange("p b (m x d) -> p b m x d", m=2, x=2)
                                act.activation(lo_part[:, p % 2], acc4[:, :, :, 1, :], ACT.Copy,
                                               scale=1.0 / LO_SCALE).then_inc(lo_taken, 1)
                            compare(hp, s, g + 1, 2)
                            compare(hp, s, g + 1, 3)

            @block.vector
            def _(dve):
                def compare(hp, s, g, c):
                    hs, gs = (s + (g // NG)) % 2, g % NG
                    n = ((2 * hp + s) * NG + g) * C + c
                    dve.wait_ge(masks_used, n + 1)
                    dve.wait_ge(arow_loaded[gs % 2], 16 * ((2 * hp + s) * (NG // 2) + g // 2 + 1))
                    dve.tensor_scalar(m1[:, c % M1_SLOTS, J - 1, :].bitcast(U8), arow[:, gs % 2, :],
                                      pack[:, hs, c * J + J - 1:c * J + J], 255.0, ALU.is_gt, ALU.mult
                                      ).then_inc(above_dve, 1)

                def adj_bits(g, c):
                    return adjT[:, c * J:(c + 1) * J, (g % NG) * GI:(g % NG + 1) * GI].bitcast(U32)

                def mask1(hp, s, g, c):
                    grp = (2 * hp + s) * NG + g
                    n = grp * C + c
                    if c in ON_DVE:
                        compare(hp, s, g, c)
                        dve.wait_ge(above_dve, grp * len(ON_DVE) + ON_DVE.index(c) + 1)
                    dve.wait_ge(above_act, n + 1)
                    m = m1[:, c % M1_SLOTS].bitcast(U32)
                    dve.tensor_tensor(m, m, adj_bits(g, c), ALU.bitwise_and).then_inc(m1_made, 1)

                def mask0(hp, s, g, c):
                    n = ((2 * hp + s) * NG + g) * C + c
                    dve.wait_ge(m1_made, n + 2)
                    dve.wait_ge(masks_used, n + 1 + M1_SLOTS - M0_SLOTS)
                    dve.tensor_tensor(m0[:, c % M0_SLOTS].bitcast(U32), m1[:, c % M1_SLOTS].bitcast(U32),
                                      adj_bits(g, c), ALU.bitwise_xor).then_inc(m0_made, 1)

                def prepare(q, slot, qq, e):
                    E = pack[:, slot, (e + 1) * T + qq * QT:(e + 1) * T + (qq + 1) * QT]
                    dve.wait_ge(seq_loaded, 16 * (q + 1))
                    if not isinstance(q, int) or q:
                        dve.wait_ge(vals_made, 2 * q + e - 1)
                    dve.tensor_tensor(prod[:, e], seq1[:], E.unsqueeze(2).to_broadcast([P, QT, DC]), ALU.mult
                                      ).then_inc(prod_made, 1)

                def lo(q, slot, qq, e):
                    v = vals[:, slot, qq * QT:(qq + 1) * QT, e]
                    dve.wait_ge(prod_made, 2 * q + e + 1)
                    dve.wait_ge(hi_made, 2 * q + e + 1)
                    dve.scalar_tensor_tensor(v[:, :, 1, :], v[:, :, 0, :], -LO_SCALE, prod[:, e], ALU.mult, ALU.add
                                             ).then_inc(vals_made, 1)

                def take(n, p):
                    acc4 = acc[:, 2 * p:2 * p + 2, 0:NV].rearrange("p b (m x d) -> p b m x d", m=2, x=2)
                    dve.wait_ge(lo_taken, 4 * n + p + 1)
                    dve.tensor_tensor(side[:, 2 * p:2 * p + 2], lo_part[:, p % 2], acc4[:, :, :, 0, :], ALU.add
                                      ).then_inc(acc_free, 1)

                dve.sem_inc(m1_made, 1)
                dve.sem_inc(hid_made, 1)
                dve.memset(seq1[:, :, DH:DC], 1.0).then_inc(ones_made, 1)
                dve.wait_ge(ones_made, 1)
                dve.wait_ge(pack_loaded[0], 16)
                for q in range(NG):
                    for e in range(2):
                        prepare(q, 0, q, e)
                    for e in range(2):
                        lo(q, 0, q, e)
                for c in range(C // 2):
                    mask1(0, 0, 0, c)
                    if c < M0_SLOTS:
                        mask0(0, 0, 0, c)
                for c in range(M0_SLOTS, C // 2):
                    mask0(0, 0, 0, c)
                with dve.Fori(0, H // 2) as hp:
                    for s in range(2):
                        for g in range(NG):
                            n = (2 * hp + s) * NG + g
                            if g == 0:
                                dve.wait_ge(pack_loaded[1 - s], 16 * (hp + 1 + s))
                            for k, c in enumerate(range(C // 2, C)):
                                mask1(hp, s, g, c)
                                if k == 0:
                                    prepare(n + NG, 1 - s, g, 0)
                                if k == 1:
                                    prepare(n + NG, 1 - s, g, 1)
                                mask0(hp, s, g, c)
                                if k == 2:
                                    lo(n + NG, 1 - s, g, 0)
                                if k == 3:
                                    lo(n + NG, 1 - s, g, 1)
                            mask1(hp, s, g + 1, 0)
                            mask0(hp, s, g + 1, 0)
                            mask1(hp, s, g + 1, 1)
                            dve.wait_ge(hid_stored, 16 * (n + 1))
                            for p in range(IG // 2):
                                take(n, p)
                            mask0(hp, s, g + 1, 1)
                            F = pack[:, s, 3 * T + 2 * IG * g:3 * T + 2 * IG * (g + 1)]
                            dve.wait_ge(acc_free, 4 * n + 8)
                            side_m = side[:].rearrange("p b m d -> p (b m) d")
                            dve.tensor_tensor(side_m, side_m, F.unsqueeze(2).to_broadcast([P, 2 * IG, DC]),
                                              ALU.mult).then_inc(sides_scaled, 1)
                            mask1(hp, s, g + 1, 2)
                            dve.wait_ge(sides_scaled, n + 1)
                            dve.tensor_tensor(both, side[:, :, 0, :], side[:, :, 1, :], ALU.add
                                              ).then_inc(both_made, 1)
                            mask0(hp, s, g + 1, 2)
                            dve.wait_ge(both_made, n + 1)
                            dve.reciprocal(rden[:], both[:, :, DH:DC]).then_inc(rden_made, 1)
                            mask1(hp, s, g + 1, 3)
                            dve.wait_ge(rden_made, n + 1)
                            dve.tensor_tensor(hid, both[:, :, 0:DH], rden[:].to_broadcast([P, IG, DH]), ALU.mult
                                              ).then_inc(hid_made, 1)
                            mask0(hp, s, g + 1, 3)

            @block.tensor
            def _(pe):
                pe.sem_inc(masks_used, M1_SLOTS)
                with pe.Fori(0, H // 2) as hp:
                    for s in range(2):
                        with pe.Fori(0, NG) as g:
                            n = (2 * hp + s) * NG + g
                            pe.wait_ge(vals_made, 2 * NG * (2 * hp + s + 1))
                            for c in range(C):
                                pe.wait_ge(m0_made, C * n + c + 1)
                                pe.sem_inc(waits_passed, 1)
                                for j in range(J):
                                    v = vals[:, s, c * J + j].rearrange("p m x d -> p m (x d)")
                                    first, last = c == 0 and j == 0, c == C - 1 and j == J - 1
                                    for t in range(IG):
                                        if first and t % 2 == 0:
                                            pe.wait_ge(acc_free, 4 * n + t // 2 + 1)
                                            pe.sem_inc(waits_passed, 1)
                                        for m, mask in enumerate((m1, m0)):
                                            slot = c % (M0_SLOTS if m else M1_SLOTS)
                                            i = pe.matmul(acc[:, t, m * 2 * DC:(m + 1) * 2 * DC],
                                                          mask[:, slot, j, t * P:(t + 1) * P], v[:, m, :],
                                                          start=first and m == 0, stop=last and m == 1,
                                                          skip_group_check=True)
                                        if last and t % 2 == 1 and t < IG - 1:
                                            i.then_inc(acc_done, 1)
                                i.then_inc(masks_used, 1)
                pe.wait_ge(masks_used, M1_SLOTS + C * NG * H)
                pe.sem_inc(masks_used, C // 2)

    def output():
        with ExitStack() as ctx:
            sb, ps, sem = tools(ctx)
            w = sb("w_out_sb", [P, K, D], F32)
            h_in = sb("h_in", [P, 2, D], F32)
            x_in = sb("x_in_o", [P, 2, D], F32)
            bias = sb("bias", [P, D], F32)
            ident = sb("ident_o", [P, P], F32)
            hT = sb("hT_o", [P, 2, K, P], F32)
            y = sb("y", [P, D], F32)
            low = sb("low", [P, D], F32)
            ex = sb("ex", [P, 2, D], F32)
            high = sb("high", [P, D], F32)
            res = sb("res", [P, 2, D], F32)
            hT_ps = ps("hT_ps", [P, K, P], F32)
            y_ps = ps("y_ps_o", [P, 2, D], F32)
            w_loaded, bias_loaded = sem("w_out_loaded"), sem("bias_loaded")
            h_loaded = [sem(f"h_loaded{n}") for n in range(2)]
            x_loaded = [sem(f"x_loaded_o{n}") for n in range(2)]
            zeroed, ident_made = sem("zeroed_o"), sem("ident_made_o")
            turned = sem("turned")
            hT_made = sem("hT_made_o")
            y_done = sem("y_done_o")
            y_taken = sem("y_taken")
            low_made, ex_made, high_made = sem("low_made"), sem("ex_made"), sem("high_made")
            res_made = sem("res_made")
            out_stored = [sem(f"out_stored{n}") for n in range(2)]
            block = ctx.enter_context(nc.Block())

            @block.sync
            def _(sp):
                def load_h(t, s):
                    sp.wait_ge(turned, 2 * t + 2)
                    sp.dma_start(h_in[:, s, :], hid_d[bass.ts(t % T, P), :]).then_inc(h_loaded[s], 16)

                load_h(0, 0)
                sp.dma_start(w[:], w_out.rearrange("(k p) n -> p k n", p=P)).then_inc(w_loaded, 16)
                sp.dma_start(bias[:], b_out.partition_broadcast(P)).then_inc(bias_loaded, 16)
                with sp.Fori(0, T // 2) as tp:
                    for s in range(2):
                        t = 2 * tp + s
                        load_h(t + 1, 1 - s)
                        sp.wait_ge(res_made, t + 1)
                        sp.dma_start(x_in[:, s, :], x[bass.ts(t, P), :]).then_inc(x_loaded[s], 16)

            @block.gpsimd
            def _(pool):
                identity(pool, ident, zeroed, ident_made)

            @block.tensor
            def _(pe):
                def turn(t, s):
                    pe.wait_ge(h_loaded[s], 16 * (t // 2 + 1))
                    pe.wait_ge(hT_made, 2 * t + 2)
                    for k in range(K):
                        i = pe.transpose(hT_ps[:, k, :], h_in[:, s, k * P:(k + 1) * P], ident[:])
                        if k % (K // 2) == K // 2 - 1:
                            i.then_inc(turned, 1)

                pe.sem_inc(turned, 4)
                pe.sem_inc(y_done, 2)
                pe.wait_ge(ident_made, 1)
                turn(0, 0)
                pe.wait_ge(w_loaded, 16)
                with pe.Fori(0, T // 2) as tp:
                    for s in range(2):
                        t = 2 * tp + s
                        pe.wait_ge(y_taken, t + 1)
                        for k in range(K):
                            if k % (K // 2) == 0:
                                pe.wait_ge(hT_made, 2 * t + 2 * k // K + 3)
                            if k == K // 2:
                                turn(t + 1, 1 - s)
                            for n in range(NY):
                                i = pe.matmul(y_ps[:, s, n * BANK:(n + 1) * BANK], hT[:, s, k, :],
                                              w[:, k, n * BANK:(n + 1) * BANK], start=k == 0, stop=k == K - 1)
                        i.then_inc(y_done, 1)

            @block.scalar
            def _(act):
                def take_h(t, s):
                    act.wait_ge(y_done, t + 1)
                    for n in range(2):
                        act.wait_ge(turned, 2 * t + n + 5)
                        act.activation(hT[:, s, n * K // 2:(n + 1) * K // 2, :],
                                       hT_ps[:, n * K // 2:(n + 1) * K // 2, :], ACT.Copy).then_inc(hT_made, 1)

                act.sem_inc(hT_made, 2)
                for n in range(2):
                    act.sem_inc(out_stored[n], 16)
                take_h(0, 0)
                with act.Fori(0, T // 2) as tp:
                    for s in range(2):
                        t = 2 * tp + s
                        take_h(t + 1, 1 - s)
                        act.wait_ge(low_made, t + 1)
                        act.activation(ex[:, s, :], low[:], ACT.Exp).then_inc(ex_made, 1)
                        act.wait_ge(res_made, t + 3)
                        act.dma_start(out[bass.ts(t, P), :], res[:, s, :]).then_inc(out_stored[s], 16)
                for n in range(2):
                    act.wait_ge(out_stored[n], 16 * (T // 2 + 1))

            @block.vector
            def _(dve):
                dve.sem_inc(y_taken, 2)
                dve.sem_inc(res_made, 2)
                dve.wait_ge(bias_loaded, 16)
                with dve.Fori(0, T // 2) as tp:
                    for s in range(2):
                        t = 2 * tp + s
                        dve.wait_ge(y_done, t + 3)
                        dve.tensor_tensor(y[:], y_ps[:, s, :], bias[:], ALU.add).then_inc(y_taken, 1)
                        dve.wait_ge(y_taken, t + 3)
                        dve.tensor_scalar(low[:], y[:], 0.0, None, ALU.min).then_inc(low_made, 1)
                        dve.wait_ge(x_loaded[s], 16 * (tp + 1))
                        dve.wait_ge(res_made, t + 2)
                        dve.scalar_tensor_tensor(high[:], y[:], 0.0, x_in[:, s, :], ALU.max, ALU.add
                                                 ).then_inc(high_made, 1)
                        dve.wait_ge(ex_made, t + 1)
                        dve.wait_ge(high_made, t + 1)
                        dve.wait_ge(out_stored[s], 16 * (tp + 1))
                        dve.scalar_tensor_tensor(res[:, s, :], ex[:, s, :], -1.0, high[:], ALU.add, ALU.add
                                                 ).then_inc(res_made, 1)

    with ExitStack() as ctx:
        adjT = ctx.enter_context(nc.sbuf_tensor("adjT", [P, T, N], U8))
        with ExitStack() as inner:
            A = inner.enter_context(nc.sbuf_tensor("A", [P, T, H], F32))
            B = inner.enter_context(nc.sbuf_tensor("B", [P, T, H], F32))
            project(adjT, A, B)
            factors(A, B)
        attend(adjT)
    output()


_INS = ["x", "adj", "L0_gnn_W_seq", "L0_gnn_a1", "L0_gnn_a2", "L0_gnn_W_out", "L0_gnn_b_out"]


def kernel(**inputs):
    import numpy as _np
    import concourse.bacc as _bacc
    from concourse import mybir as _mybir
    from concourse.bass_utils import run_bass_kernel_spmd as _run

    nc = _bacc.Bacc("TRN2", target_bir_lowering=False, num_devices=1)
    arrays, args = {}, []
    for name in _INS:
        a = _np.ascontiguousarray(inputs[name])
        arrays[f"in_{name}"] = a
        args.append(nc.dram_tensor(f"in_{name}", a.shape, _mybir.dt.from_np(a.dtype), kind="ExternalInput").ap())
    out = nc.dram_tensor("out_0", inputs["x"].shape, _mybir.dt.float32, kind="ExternalOutput").ap()
    build(nc, *args, out)
    r = _run(nc, [arrays], core_ids=[0])
    return r.results[0]["out_0"]
```

```python
from contextlib import ExitStack

import concourse.bass as bass
from concourse import mybir

F32 = mybir.dt.float32
F16 = mybir.dt.float16
BF16 = mybir.dt.bfloat16
F8 = mybir.dt.float8e4
U8 = mybir.dt.uint8
I8 = mybir.dt.int8
U32 = mybir.dt.uint32
ALU = mybir.AluOpType
ACT = mybir.ActivationFunctionType
AX_X = mybir.AxisListType.X
RMAX = bass.bass_isa.ReduceOp.max

P = 128
ALPHA = 0.2
EPS = 1e-5
EDGE = 0xC0
TOP_BITS = 0x80808080
LO_SCALE = 4096.0
X_SCALE = 64.0
W_SCALE = 1024.0
E_SCALE = 64.0


def build(nc, x, adj, w_seq, a1, a2, w_out, b_out, out):
    N, D = x.shape
    DH = a1.shape[0]
    H = D // DH
    T = N // P
    K = D // P
    BANK = 512
    NY = D // BANK
    Q = 4
    QJ = T // Q

    IG = 8
    GI = IG * P
    NG = T // IG
    J = 4
    C = T // J
    M1_SLOTS, M0_SLOTS = 4, 2
    DC = DH + 1
    NV = 4 * DC
    QT = T // NG
    PK = 5 * T
    ON_DVE = (1, 1, 2, 1, 1, 1, 1, 1)
    assert T % IG == 0 and QT * NG == T and NV <= BANK

    seq_d = nc.dram_tensor("seq_by_head", (H, P, T, DH), F32, kind="Internal").ap()
    pack_d = nc.dram_tensor("pack_by_head", (H, P, PK), F32, kind="Internal").ap()
    arow_d = nc.dram_tensor("a_by_head", (H, N), F32, kind="Internal").ap()
    hid_d = nc.dram_tensor("hidden", (N, D), F32, kind="Internal").ap()

    def tools(ctx):
        return (lambda name, shape, dt: ctx.enter_context(nc.sbuf_tensor(name, shape, dt)),
                lambda name, shape, dt: ctx.enter_context(nc.psum_tensor(name, shape, dt)),
                lambda name: ctx.enter_context(nc.semaphore(name)))

    def split_weights(sp, act, dve, dram, stage, whi, wlo, loaded, hi_made, lo_made):
        slots = stage.shape[1]
        for k in range(K):
            s = k % slots
            if sp:
                if k >= slots:
                    sp.wait_ge(lo_made, k - slots + 1)
                sp.dma_start(stage[:, s, :], dram[k * P:(k + 1) * P, :]).then_inc(loaded[s], 16)
            if act:
                act.wait_ge(loaded[s], 16 * (k // slots + 1))
                act.activation(whi[:, k, :], stage[:, s, :], ACT.Copy, scale=W_SCALE).then_inc(hi_made, 1)
            if dve:
                dve.wait_ge(hi_made, k + 1)
                dve.scalar_tensor_tensor(wlo[:, k, :], stage[:, s, :], W_SCALE, whi[:, k, :], ALU.mult,
                                         ALU.subtract).then_inc(lo_made, 1)

    def multiply(pe, y, hT, whi, wlo, k, n):
        cols = slice(n * BANK, (n + 1) * BANK)
        pe.matmul(y[:, cols], hT[:, 0, k, :], whi[:, k, cols], start=k == 0, stop=False)
        pe.matmul(y[:, cols], hT[:, 0, k, :], wlo[:, k, cols], start=False, stop=False)
        return pe.matmul(y[:, cols], hT[:, 1, k, :], whi[:, k, cols], start=False, stop=k == K - 1)

    def identity(pool, tile, zeroed, made):
        pool.memset(tile[:], 0.0).then_inc(zeroed, 1)
        pool.wait_ge(zeroed, 1)
        pool.affine_select(out=tile[:], in_=tile[:], compare_op=ALU.not_equal, fill=1.0, base=0,
                           pattern=[[-1, P]], channel_multiplier=1).then_inc(made, 1)

    def project(adjT, A, B):
        with ExitStack() as ctx:
            sb, ps, sem = tools(ctx)
            whi = sb("w_seq_hi", [P, K, D], F16)
            wlo = sb("w_seq_lo", [P, K, D], F16)
            x_in = sb("x_in", [P, D], F32)
            xn = sb("xn", [P, D], F32)
            hT = sb("hT", [P, 2, 2, K, P], F16)
            seq = sb("seq", [P, H, DH], F32)
            prod = sb("prod", [P, H, DH], F32)
            adj_in = sb("adj_in", [P, Q, QJ * P], F32)
            ident = sb("ident", [P, P], F32)
            ident16 = sb("ident16", [P, P], BF16)
            a12 = sb("a12", [P, 2, DH], F32)
            stats = sb("stats", [P, 2, 6], F32)
            mv = sb("mv", [P, 2], F32)
            var = sb("var", [P, 1], F32)
            std = sb("std", [P, 1], F32)
            rstd = sb("rstd", [P, 1], F32)
            xT_ps = ps("xT_ps", [P, K, P], F32)
            y_ps = ps("y_ps", [P, 2, D], F32)
            adj_ps = ps("adj_ps", [P, 2, QJ, P], BF16)

            w_loaded = [sem(f"w_loaded{n}") for n in range(Q)]
            whi_made, wlo_made = sem("whi_made"), sem("wlo_made")
            hi_made = sem("hT_hi_made")
            a12_loaded = sem("a12_loaded")
            x_loaded = sem("x_loaded")
            adj_loaded = [sem(f"adj_loaded{q}") for q in range(Q)]
            adj_turned = sem("adj_turned")
            adj_bank_free = sem("adj_bank_free")
            zeroed, zeroed16 = sem("zeroed"), sem("zeroed16")
            ident_made = sem("ident_made")
            stats_made = sem("stats_made")
            stats_seen = sem("stats_seen")
            mv_made = sem("mv_made")
            var_made = sem("var_made")
            std_made = sem("std_made")
            rstd_made = sem("rstd_made")
            xn_made = sem("xn_made")
            xT_done = sem("xT_done")
            hT_made = sem("hT_made")
            y_done = sem("y_done")
            seq_made = sem("seq_made")
            seq_stored = sem("seq_stored")
            prod_made = sem("prod_made")
            score_made = sem("score_made")
            block = ctx.enter_context(nc.Block())

            @block.sync
            def _(sp):
                sp.dma_start(x_in[:], x[0:P, :]).then_inc(x_loaded, 16)
                sp.dma_start(a12[:, 0, :], a1.partition_broadcast(P)).then_inc(a12_loaded, 16)
                sp.dma_start(a12[:, 1, :], a2.partition_broadcast(P)).then_inc(a12_loaded, 16)
                split_weights(sp, None, None, w_seq, adj_in, whi, wlo, w_loaded, whi_made, wlo_made)
                sp.wait_ge(xn_made, 2)
                sp.dma_start(x_in[:], x[P:2 * P, :]).then_inc(x_loaded, 16)
                sp.wait_ge(wlo_made, K)
                with sp.Fori(0, T) as t:
                    for q in range(Q):
                        sp.wait_ge(adj_turned, Q * t + q + 1)
                        sp.dma_start(adj_in[:, q, :], adj[bass.ts(t, P), q * QJ * P:(q + 1) * QJ * P]
                                     ).then_inc(adj_loaded[q], 16)
                    sp.wait_ge(xn_made, t + 3)
                    sp.dma_start(x_in[:], x[bass.ts((t + 2) % T, P), :]).then_inc(x_loaded, 16)

            @block.gpsimd
            def _(pool):
                identity(pool, ident, zeroed, ident_made)
                identity(pool, ident16, zeroed16, ident_made)

            @block.vector
            def _(dve):
                def norm(t):
                    dve.wait_ge(x_loaded, 16 * (t + 1))
                    for n in range(2):
                        dve.bn_stats(stats[:, n, :], x_in[:, n * D // 2:(n + 1) * D // 2]).then_inc(stats_made, 1)
                    dve.wait_ge(stats_made, 2 * (t + 1))
                    dve.sem_inc(stats_seen, 1)
                    dve.wait_ge(xn_made, t + 1)
                    dve.sem_inc(stats_seen, 1)
                    dve.bn_aggr(mv[:], stats[:]).then_inc(mv_made, 1)
                    dve.wait_ge(mv_made, t + 1)
                    dve.tensor_scalar(var[:], mv[:, 1:2], EPS, None, ALU.add).then_inc(var_made, 1)
                    dve.wait_ge(std_made, t + 1)
                    dve.reciprocal(rstd[:], std[:]).then_inc(rstd_made, 1)
                    dve.wait_ge(rstd_made, t + 1)
                    dve.wait_ge(xT_done, 2 * t + 1)
                    dve.tensor_scalar(xn[:], x_in[:], mv[:, 0:1], rstd[:], ALU.subtract, ALU.mult
                                      ).then_inc(xn_made, 1)

                dve.sem_inc(seq_made, 2)
                dve.sem_inc(hT_made, 2)
                dve.sem_inc(xn_made, 1)
                dve.sem_inc(score_made, 1)
                def take_lo(t, s):
                    for n in range(2):
                        ks = slice(n * K // 2, (n + 1) * K // 2)
                        dve.wait_ge(hi_made, 2 * t + n + 1)
                        dve.scalar_tensor_tensor(hT[:, s, 1, ks, :], xT_ps[:, ks, :], 0.0, hT[:, s, 0, ks, :],
                                                 ALU.max, ALU.subtract).then_inc(hT_made, 1)

                norm(0)
                split_weights(None, None, dve, w_seq, adj_in, whi, wlo, w_loaded, whi_made, wlo_made)
                take_lo(0, 0)
                norm(1)
                dve.wait_ge(a12_loaded, 32)
                with dve.Fori(0, T // 2) as tp:
                    for s in range(2):
                        t = 2 * tp + s
                        take_lo(t + 1, 1 - s)
                        dve.wait_ge(y_done, t + 3)
                        dve.wait_ge(seq_stored, 16 * (t + 1))
                        dve.tensor_scalar(seq[:].rearrange("p h d -> p (h d)"), y_ps[:, s, :],
                                          1.0 / (X_SCALE * W_SCALE), None, ALU.mult).then_inc(seq_made, 1)
                        norm(t + 2)
                        dve.wait_ge(seq_made, t + 3)
                        for n, S in enumerate((A, B)):
                            dve.wait_ge(score_made, 2 * t + n + 1)
                            dve.tensor_tensor(prod[:], seq[:],
                                              a12[:, n:n + 1, :].to_broadcast([P, H, DH]), ALU.mult
                                              ).then_inc(prod_made, 1)
                            dve.wait_ge(prod_made, 2 * t + n + 1)
                            dve.tensor_reduce(S[:, bass.ds(t, 1), :], prod[:], AX_X, ALU.add
                                              ).then_inc(score_made, 1)

            @block.scalar
            def _(act):
                def root(t):
                    act.wait_ge(var_made, t + 1)
                    act.activation(std[:], var[:], ACT.Sqrt, scale=X_SCALE ** -2).then_inc(std_made, 1)

                def take_h(t, s):
                    act.wait_ge(y_done, t + 1)
                    for n in range(2):
                        act.wait_ge(xT_done, 2 * t + n + 2)
                        act.activation(hT[:, s, 0, n * K // 2:(n + 1) * K // 2, :],
                                       xT_ps[:, n * K // 2:(n + 1) * K // 2, :], ACT.Relu
                                       ).then_inc(hi_made, 1)

                def take_adj(t, q):
                    act.wait_ge(adj_turned, Q * (t + 1) + q + 1)
                    act.activation(adjT[:, q * QJ:(q + 1) * QJ, bass.ts(t, P)], adj_ps[:, q % 2, :, :],
                                   ACT.Copy, scale=float(EDGE)).then_inc(adj_bank_free, 1)

                act.sem_inc(adj_bank_free, 2)
                act.sem_inc(seq_stored, 16)
                root(0)
                split_weights(None, act, None, w_seq, adj_in, whi, wlo, w_loaded, whi_made, wlo_made)
                take_h(0, 0)
                root(1)
                with act.Fori(0, T // 2) as tp:
                    for s in range(2):
                        t = 2 * tp + s
                        take_h(t + 1, 1 - s)
                        for q in range(Q):
                            take_adj(t, q)
                        root(t + 2)
                        act.wait_ge(seq_made, t + 3)
                        act.dma_start(seq_d[:, :, bass.ds(t, 1), :].rearrange("h p t d -> p h (t d)"), seq[:]
                                      ).then_inc(seq_stored, 16)
                act.wait_ge(seq_stored, 16 * (T + 1))

            @block.tensor
            def _(pe):
                def turn_x(t):
                    pe.wait_ge(xn_made, t + 2)
                    pe.wait_ge(hT_made, 2 * t + 2)
                    for k in range(K):
                        i = pe.transpose(xT_ps[:, k, :], xn[:, k * P:(k + 1) * P], ident[:])
                        if k % (K // 2) == K // 2 - 1:
                            i.then_inc(xT_done, 1)

                def turn_adj(t, q):
                    pe.wait_ge(adj_loaded[q], 16 * (t + 1))
                    pe.wait_ge(adj_bank_free, Q * t + q + 1)
                    upper = adj_in[:, q, :].bitcast(BF16).rearrange("p (j c two) -> p j c two", j=QJ, two=2)
                    for j in range(QJ):
                        i = pe.transpose(adj_ps[:, q % 2, j, :], upper[:, j, :, 1], ident16[:])
                    i.then_inc(adj_turned, 1)

                pe.sem_inc(y_done, 2)
                pe.sem_inc(adj_turned, Q)
                pe.sem_inc(xT_done, 1)
                pe.wait_ge(ident_made, 2)
                turn_x(0)
                with pe.Fori(0, T // 2) as tp:
                    for s in range(2):
                        t = 2 * tp + s
                        pe.wait_ge(seq_made, t + 1)
                        for k in range(K):
                            if k % (K // 2) == 0:
                                pe.wait_ge(hT_made, 2 * t + 2 * k // K + 3)
                            if k == K // 2:
                                turn_x(t + 1)
                            if k >= K - Q:
                                turn_adj(t, k - K + Q)
                            pe.wait_ge(wlo_made, k + 1)
                            for n in range(NY):
                                i = multiply(pe, y_ps[:, s], hT[:, s], whi, wlo, k, n)
                        i.then_inc(y_done, 1)

    def factors(A, B):
        with ExitStack() as ctx:
            sb, ps, sem = tools(ctx)
            ident = sb("ident_f", [P, P], F32)
            top = sb("top", [P, H], F32)
            bmax = sb("bmax", [P, H], F32)
            diff = sb("diff", [P, H, T], F32)
            z = sb("z", [P, H, T], F32)
            zlo = sb("zlo", [P, H, T], F32)
            zhi = sb("zhi", [P, H, T], F32)
            e = sb("e", [P, 2, H, T], F32)
            pack = sb("pack", [P, H, PK], F32)
            aT = sb("aT", [H, N], F32)
            aT_ps = ps("aT_ps", [P, 2, BANK], F32)
            zeroed, ident_made = sem("zeroed_f"), sem("ident_made_f")
            top_made, bmax_made = sem("top_made"), sem("bmax_made")
            args_made = sem("args_made")
            e_made, pack_made = sem("e_made"), sem("pack_made")
            aT_done, aT_taken = sem("aT_done"), sem("aT_taken")
            stored = sem("factors_stored")
            block = ctx.enter_context(nc.Block())

            @block.gpsimd
            def _(pool):
                identity(pool, ident, zeroed, ident_made)
                pool.wait_ge(top_made, 1)
                pool.partition_all_reduce(bmax[:], top[:], P, RMAX).then_inc(bmax_made, 1)

            @block.vector
            def _(dve):
                def heads_first(S):
                    return S[:].rearrange("p t h -> p h t")

                dve.tensor_reduce(top[:], heads_first(B), AX_X, ALU.max).then_inc(top_made, 1)
                dve.tensor_scalar(pack[:, :, 0:T], heads_first(B), -1.0, None, ALU.mult).then_inc(pack_made, 1)
                dve.wait_ge(bmax_made, 1)
                wide = bmax[:].unsqueeze(2).to_broadcast([P, H, T])
                dve.tensor_tensor(diff[:], heads_first(B), wide, ALU.subtract).then_inc(args_made, 1)
                dve.tensor_tensor(z[:], heads_first(A), wide, ALU.add).then_inc(args_made, 1)
                dve.wait_ge(args_made, 2)
                dve.tensor_scalar(zlo[:], z[:], 0.0, 1.0 - ALPHA, ALU.min, ALU.mult).then_inc(args_made, 1)
                dve.tensor_scalar(zhi[:], z[:], 0.0, ALPHA - 1.0, ALU.max, ALU.mult).then_inc(args_made, 1)
                dve.wait_ge(e_made, 2)
                for n in range(2):
                    dve.tensor_scalar(pack[:, :, (n + 1) * T:(n + 2) * T], e[:, n, :, :], E_SCALE * LO_SCALE,
                                      None, ALU.mult).then_inc(pack_made, 1)

            @block.tensor
            def _(pe):
                pe.wait_ge(ident_made, 1)
                for g in range(T // 4):
                    if g >= 2:
                        pe.wait_ge(aT_taken, g - 1)
                    for n in range(4):
                        i = pe.transpose(aT_ps[0:H, g % 2, n * P:(n + 1) * P], A[:, 4 * g + n, :], ident[:])
                    i.then_inc(aT_done, 1)

            @block.scalar
            def _(act):
                for g in range(T // 4):
                    act.wait_ge(aT_done, g + 1)
                    act.activation(aT[:, g * BANK:(g + 1) * BANK], aT_ps[0:H, g % 2, :], ACT.Copy
                                   ).then_inc(aT_taken, 1)
                act.wait_ge(args_made, 4)
                act.activation(e[:, 0], diff[:], ACT.Exp).then_inc(e_made, 1)
                act.activation(e[:, 1], diff[:], ACT.Exp, scale=ALPHA).then_inc(e_made, 1)
                F = pack[:, :, 3 * T:5 * T].rearrange("p h (t two) -> p h t two", two=2)
                act.activation(F[:, :, :, 0], zlo[:], ACT.Exp).then_inc(pack_made, 1)
                act.activation(F[:, :, :, 1], zhi[:], ACT.Exp).then_inc(pack_made, 1)

            @block.sync
            def _(sp):
                sp.wait_ge(aT_taken, T // 4)
                sp.dma_start(arow_d, aT[:]).then_inc(stored, 16)
                sp.wait_ge(pack_made, 5)
                sp.dma_start(pack_d.rearrange("h p c -> p h c"), pack[:]).then_inc(stored, 16)
                sp.wait_ge(stored, 32)

    def attend(adjT):
        with ExitStack() as ctx:
            sb, ps, sem = tools(ctx)
            arow = sb("arow", [P, 2, GI], F32)
            m1 = sb("m1", [P, M1_SLOTS, J, GI], F8)
            m0 = sb("m0", [P, M0_SLOTS, J, GI], F8)
            vals = sb("vals", [P, 2, T, 2, 2, DC], F16)
            pack = sb("pack_h", [P, 2, PK], F32)
            seq1 = sb("seq1", [P, QT, DC], F32)
            prod = sb("prod_v", [P, 2, QT, DC], F32)
            lo_part = sb("lo_part", [P, 2, 2, 2, DC], F32)
            side = sb("side", [P, IG, 2, DC], F32)
            both, hid = side[:, :, 0, :], side[:, :, 1, 0:DH]
            rden = sb("rden", [P, IG, 1], F32)
            acc = ps("acc", [P, IG, BANK], F32)

            pack_loaded = [sem(f"pack_loaded{n}") for n in range(2)]
            seq_loaded = sem("seq_loaded")
            arow_loaded = [sem(f"arow_loaded{n}") for n in range(2)]
            ones_made = sem("ones_made")
            prod_made = sem("prod_v_made")
            hi_made = sem("hi_made")
            vals_made = sem("vals_made")
            above_act = sem("above_act")
            above_dve = sem("above_dve")
            m1_made = sem("m1_made")
            m0_made = sem("m0_made")
            masks_used = sem("masks_used")
            waits_passed = sem("waits_passed")
            acc_done = sem("acc_done")
            lo_taken = sem("lo_taken")
            acc_free = sem("acc_free")
            sides_scaled = sem("sides_scaled")
            both_made = sem("both_made")
            rden_made = sem("rden_made")
            hid_made = sem("hid_made")
            hid_stored = sem("hid_stored")
            block = ctx.enter_context(nc.Block())

            def head(hp, s, ahead):
                return (2 * hp + s + ahead) % H

            @block.sync
            def _(sp):
                def load_seq(h, q):
                    sp.dma_start(seq1[:, :, 0:DH], seq_d[bass.ds(h, 1), :, q * QT:(q + 1) * QT, :]
                                 .rearrange("h p t d -> (h p) t d")).then_inc(seq_loaded, 16)

                def load_pack(h, slot):
                    sp.dma_start(pack[:, slot, :], pack_d[bass.ds(h, 1), :, :].rearrange("h p c -> (h p) c")
                                 ).then_inc(pack_loaded[slot], 16)

                def load_arow(h, g, slot):
                    sp.dma_start(arow[:, slot, :], arow_d[bass.ds(h, 1), g * GI:(g + 1) * GI]
                                 .rearrange("h n -> (h n)").partition_broadcast(P)).then_inc(arow_loaded[slot], 16)

                sp.sem_inc(hid_stored, 16)
                load_pack(0, 0)
                load_arow(0, 0, 0)
                for q in range(NG):
                    if q:
                        sp.wait_ge(prod_made, 2 * q)
                    load_seq(0, q)
                sp.wait_ge(prod_made, 2 * NG)
                load_seq(1, 0)
                with sp.Fori(0, H // 2) as hp:
                    for s in range(2):
                        for g in range(NG):
                            n = (2 * hp + s) * NG + g
                            if g == 0:
                                sp.wait_ge(sides_scaled, n + 1)
                                load_pack(head(hp, s, 1), 1 - s)
                            sp.wait_ge(m1_made, C * n + 1)
                            load_arow(head(hp, s, (g + 1) // NG), (g + 1) % NG, (g + 1) % 2)
                            sp.wait_ge(prod_made, 2 * (n + NG + 1))
                            load_seq(head(hp, s, 1 + (g + 1) // NG), (g + 1) % NG)
                            sp.wait_ge(hid_made, n + 2)
                            sp.dma_start(hid_d[g * GI:(g + 1) * GI, :]
                                         .rearrange("(t p) c -> p t c", p=P)[:, :, bass.ts(2 * hp + s, DH)],
                                         hid).then_inc(hid_stored, 16)
                sp.wait_ge(hid_stored, 16 * (H * NG + 1))
                sp.wait_ge(seq_loaded, 16 * (H * NG + NG + 1))
                for slot in range(2):
                    sp.wait_ge(pack_loaded[slot], 16 * (H // 2 + 1 - slot))
                    sp.wait_ge(arow_loaded[slot], 16 * (H * NG // 2 + 1 - slot))

            @block.scalar
            def _(act):
                def compare(hp, s, g, c):
                    hs, gs = (s + (g // NG)) % 2, g % NG
                    grp = (2 * hp + s) * NG + g
                    n = grp * C + c
                    act.wait_ge(masks_used, n + 1)
                    if c == 0:
                        act.wait_ge(arow_loaded[gs % 2], 16 * ((2 * hp + s) * (NG // 2) + g // 2 + 1))
                    for j in range(J - ON_DVE[c]):
                        i = act.activation(m1[:, c % M1_SLOTS, j, :].bitcast(I8), arow[:, gs % 2, :], ACT.Sign,
                                           bias=pack[:, hs, c * J + j:c * J + j + 1], scale=-1.0)
                    i.then_inc(above_act, 1)

                def hi(q, slot, qq, e):
                    act.wait_ge(prod_made, 2 * q + e + 1)
                    act.activation(vals[:, slot, qq * QT:(qq + 1) * QT, e, 0, :], prod[:, e, :, :], ACT.Copy,
                                   scale=1.0 / LO_SCALE).then_inc(hi_made, 1)

                act.wait_ge(pack_loaded[0], 16)
                act.sem_inc(acc_free, 4)
                for q in range(NG):
                    for e in range(2):
                        hi(q, 0, q, e)
                for c in range(C // 2):
                    compare(0, 0, 0, c)
                with act.Fori(0, H // 2) as hp:
                    for s in range(2):
                        for g in range(NG):
                            n = (2 * hp + s) * NG + g
                            for c in range(C // 2, C):
                                compare(hp, s, g, c)
                                if c in (C // 2 + 1, C // 2 + 2):
                                    if g == 0 and c == C // 2 + 1:
                                        act.wait_ge(masks_used, M1_SLOTS + C * n)
                                    hi(n + NG, 1 - s, g, c - C // 2 - 1)
                            if g == NG - 1:
                                act.wait_ge(pack_loaded[1 - s], 16 * (hp + 1 + s))
                            for c in range(C // 2 - 1):
                                compare(hp, s, g + 1, c)
                            for p in range(IG // 2):
                                if p < IG // 2 - 1:
                                    act.wait_ge(acc_done, 3 * n + p + 1)
                                else:
                                    act.wait_ge(masks_used, M1_SLOTS + C * (n + 1))
                                act.wait_ge(acc_free, 4 * n + p + 3)
                                acc4 = acc[:, 2 * p:2 * p + 2, 0:NV].rearrange("p b (m x d) -> p b m x d", m=2, x=2)
                                act.activation(lo_part[:, p % 2], acc4[:, :, :, 1, :], ACT.Copy,
                                               scale=1.0 / LO_SCALE).then_inc(lo_taken, 1)
                            compare(hp, s, g + 1, C // 2 - 1)

            @block.vector
            def _(dve):
                def compare(hp, s, g, c):
                    hs, gs = (s + (g // NG)) % 2, g % NG
                    n = ((2 * hp + s) * NG + g) * C + c
                    dve.wait_ge(masks_used, n + 1)
                    dve.wait_ge(arow_loaded[gs % 2], 16 * ((2 * hp + s) * (NG // 2) + g // 2 + 1))
                    for j in range(J - ON_DVE[c], J):
                        i = dve.tensor_scalar(m1[:, c % M1_SLOTS, j, :].bitcast(U8), arow[:, gs % 2, :],
                                              pack[:, hs, c * J + j:c * J + j + 1], 255.0, ALU.is_gt, ALU.mult)
                    i.then_inc(above_dve, 1)

                def adj_bits(g, c):
                    return adjT[:, c * J:(c + 1) * J, (g % NG) * GI:(g % NG + 1) * GI].bitcast(U32)

                def mask1(hp, s, g, c, between=None):
                    n = ((2 * hp + s) * NG + g) * C + c
                    dve.wait_ge(above_dve, n + 1)
                    dve.wait_ge(above_act, n + 1)
                    m = m1[:, c % M1_SLOTS].bitcast(U32)
                    dve.scalar_tensor_tensor(m, m, TOP_BITS, adj_bits(g, c), ALU.bitwise_xor, ALU.bitwise_and
                                             ).then_inc(m1_made, 1)
                    if between:
                        between()
                    compare(hp, s, g + (c + 1) // C, (c + 1) % C)

                def mask0(hp, s, g, c):
                    n = ((2 * hp + s) * NG + g) * C + c
                    dve.wait_ge(m1_made, n + 2)
                    dve.wait_ge(masks_used, n + 1 + M1_SLOTS - M0_SLOTS)
                    dve.tensor_scalar(m0[:, c % M0_SLOTS].bitcast(U32), m1[:, c % M1_SLOTS].bitcast(U32),
                                      TOP_BITS, 1, ALU.bitwise_and, ALU.logical_shift_right).then_inc(m0_made, 1)

                def prepare(q, slot, qq, e):
                    E = pack[:, slot, (e + 1) * T + qq * QT:(e + 1) * T + (qq + 1) * QT]
                    dve.wait_ge(seq_loaded, 16 * (q + 1))
                    if not isinstance(q, int) or q:
                        dve.wait_ge(vals_made, 2 * q + e - 1)
                    dve.tensor_tensor(prod[:, e], seq1[:], E.unsqueeze(2).to_broadcast([P, QT, DC]), ALU.mult
                                      ).then_inc(prod_made, 1)

                def lo(q, slot, qq, e):
                    v = vals[:, slot, qq * QT:(qq + 1) * QT, e]
                    dve.wait_ge(prod_made, 2 * q + e + 1)
                    dve.wait_ge(hi_made, 2 * q + e + 1)
                    dve.scalar_tensor_tensor(v[:, :, 1, :], v[:, :, 0, :], -LO_SCALE, prod[:, e], ALU.mult, ALU.add
                                             ).then_inc(vals_made, 1)

                def take(n, p):
                    acc4 = acc[:, 2 * p:2 * p + 2, 0:NV].rearrange("p b (m x d) -> p b m x d", m=2, x=2)
                    dve.wait_ge(lo_taken, 4 * n + p + 1)
                    dve.tensor_tensor(side[:, 2 * p:2 * p + 2], lo_part[:, p % 2], acc4[:, :, :, 0, :], ALU.add
                                      ).then_inc(acc_free, 1)

                dve.sem_inc(m1_made, 1)
                dve.sem_inc(sides_scaled, 1)
                dve.sem_inc(hid_made, 1)
                dve.memset(seq1[:, :, DH:DC], 1.0).then_inc(ones_made, 1)
                dve.wait_ge(ones_made, 1)
                dve.wait_ge(pack_loaded[0], 16)
                for q in range(NG):
                    for e in range(2):
                        prepare(q, 0, q, e)
                    for e in range(2):
                        lo(q, 0, q, e)
                compare(0, 0, 0, 0)
                for c in range(C // 2):
                    mask1(0, 0, 0, c)
                    mask0(0, 0, 0, c)
                with dve.Fori(0, H // 2) as hp:
                    for s in range(2):
                        for g in range(NG):
                            n = (2 * hp + s) * NG + g

                            def take_all():
                                dve.wait_ge(hid_stored, 16 * (n + 1))
                                for p in range(IG // 2):
                                    take(n, p)

                            def scale():
                                F = pack[:, s, 3 * T + 2 * IG * g:3 * T + 2 * IG * (g + 1)]
                                side_m = side[:].rearrange("p b m d -> p (b m) d")
                                dve.wait_ge(acc_free, 4 * n + 8)
                                dve.tensor_tensor(side_m, side_m, F.unsqueeze(2).to_broadcast([P, 2 * IG, DC]),
                                                  ALU.mult).then_inc(sides_scaled, 1)

                            def add():
                                dve.wait_ge(sides_scaled, n + 2)
                                dve.tensor_tensor(both, side[:, :, 0, :], side[:, :, 1, :], ALU.add
                                                  ).then_inc(both_made, 1)

                            def invert():
                                dve.wait_ge(both_made, n + 1)
                                dve.reciprocal(rden[:], both[:, :, DH:DC]).then_inc(rden_made, 1)

                            def divide():
                                dve.wait_ge(rden_made, n + 1)
                                dve.tensor_tensor(hid, both[:, :, 0:DH], rden[:].to_broadcast([P, IG, DH]),
                                                  ALU.mult).then_inc(hid_made, 1)

                            if g == 0:
                                dve.wait_ge(pack_loaded[1 - s], 16 * (hp + 1 + s))
                            q = n + NG
                            ahead = (lambda: prepare(q, 1 - s, g, 0), lambda: prepare(q, 1 - s, g, 1),
                                     lambda: lo(q, 1 - s, g, 0), lambda: lo(q, 1 - s, g, 1))
                            for k in range(C // 2):
                                mask1(hp, s, g, C // 2 + k, ahead[k])
                                mask0(hp, s, g, C // 2 + k)
                            mask1(hp, s, g + 1, 0)
                            mask0(hp, s, g + 1, 0)
                            mask1(hp, s, g + 1, 1, take_all)
                            mask0(hp, s, g + 1, 1)
                            scale()
                            mask1(hp, s, g + 1, 2, add)
                            mask0(hp, s, g + 1, 2)
                            invert()
                            mask1(hp, s, g + 1, 3, divide)
                            mask0(hp, s, g + 1, 3)

            @block.tensor
            def _(pe):
                pe.sem_inc(masks_used, M1_SLOTS)
                with pe.Fori(0, H // 2) as hp:
                    for s in range(2):
                        with pe.Fori(0, NG) as g:
                            n = (2 * hp + s) * NG + g
                            pe.wait_ge(vals_made, 2 * NG * (2 * hp + s + 1))
                            for c in range(C):
                                pe.wait_ge(m0_made, C * n + c + 1)
                                pe.sem_inc(waits_passed, 1)
                                for t in range(IG):
                                    if c == 0 and t % 2 == 0:
                                        pe.wait_ge(acc_free, 4 * n + t // 2 + 1)
                                        pe.sem_inc(waits_passed, 1)
                                    for j in range(J):
                                        v = vals[:, s, c * J + j].rearrange("p m x d -> p m (x d)")
                                        first, last = c == 0 and j == 0, c == C - 1 and j == J - 1
                                        for m, mask in enumerate((m1, m0)):
                                            slot = c % (M0_SLOTS if m else M1_SLOTS)
                                            i = pe.matmul(acc[:, t, m * 2 * DC:(m + 1) * 2 * DC],
                                                          mask[:, slot, j, t * P:(t + 1) * P], v[:, m, :],
                                                          start=first and m == 0, stop=last and m == 1,
                                                          skip_group_check=True)
                                    if c == C - 1 and t % 2 == 1 and t < IG - 1:
                                        i.then_inc(acc_done, 1)
                                i.then_inc(masks_used, 1)
                pe.wait_ge(masks_used, M1_SLOTS + C * NG * H)
                pe.sem_inc(masks_used, C // 2)

    def output():
        with ExitStack() as ctx:
            sb, ps, sem = tools(ctx)
            whi = sb("w_out_hi", [P, K, D], F16)
            wlo = sb("w_out_lo", [P, K, D], F16)
            stage = sb("w_out_stage", [P, 4, D], F32)
            h_in = sb("h_in", [P, 2, D], F32)
            x_in = sb("x_in_o", [P, 2, D], F32)
            bias = sb("bias", [P, D], F32)
            ident = sb("ident_o", [P, P], F32)
            hT = sb("hT_o", [P, 2, 2, K, P], F16)
            y = sb("y", [P, D], F32)
            low = sb("low", [P, D], F32)
            ex = sb("ex", [P, 2, D], F32)
            high = sb("high", [P, D], F32)
            res = sb("res", [P, 2, D], F32)
            hT_ps = ps("hT_ps", [P, K, P], F32)
            y_ps = ps("y_ps_o", [P, 2, D], F32)
            w_loaded = [sem(f"w_out_loaded{n}") for n in range(4)]
            whi_made, wlo_made = sem("w_out_hi_made"), sem("w_out_lo_made")
            hi_made = sem("hT_hi_made_o")
            bias_loaded = sem("bias_loaded")
            h_loaded = [sem(f"h_loaded{n}") for n in range(2)]
            x_loaded = [sem(f"x_loaded_o{n}") for n in range(2)]
            zeroed, ident_made = sem("zeroed_o"), sem("ident_made_o")
            turned = sem("turned")
            hT_made = sem("hT_made_o")
            y_done = sem("y_done_o")
            y_taken = sem("y_taken")
            low_made, ex_made, high_made = sem("low_made"), sem("ex_made"), sem("high_made")
            res_made = sem("res_made")
            out_stored = [sem(f"out_stored{n}") for n in range(2)]
            block = ctx.enter_context(nc.Block())

            @block.sync
            def _(sp):
                def load_h(t, s):
                    sp.wait_ge(turned, 2 * t + 2)
                    sp.dma_start(h_in[:, s, :], hid_d[bass.ts(t % T, P), :]).then_inc(h_loaded[s], 16)

                load_h(0, 0)
                split_weights(sp, None, None, w_out, stage, whi, wlo, w_loaded, whi_made, wlo_made)
                sp.dma_start(bias[:], b_out.partition_broadcast(P)).then_inc(bias_loaded, 16)
                with sp.Fori(0, T // 2) as tp:
                    for s in range(2):
                        t = 2 * tp + s
                        load_h(t + 1, 1 - s)
                        sp.wait_ge(res_made, t + 1)
                        sp.dma_start(x_in[:, s, :], x[bass.ts(t, P), :]).then_inc(x_loaded[s], 16)

            @block.gpsimd
            def _(pool):
                identity(pool, ident, zeroed, ident_made)

            @block.tensor
            def _(pe):
                def turn(t, s):
                    pe.wait_ge(h_loaded[s], 16 * (t // 2 + 1))
                    pe.wait_ge(hT_made, 2 * t + 2)
                    for k in range(K):
                        i = pe.transpose(hT_ps[:, k, :], h_in[:, s, k * P:(k + 1) * P], ident[:])
                        if k % (K // 2) == K // 2 - 1:
                            i.then_inc(turned, 1)

                pe.sem_inc(turned, 4)
                pe.sem_inc(y_done, 2)
                pe.wait_ge(ident_made, 1)
                turn(0, 0)
                with pe.Fori(0, T // 2) as tp:
                    for s in range(2):
                        t = 2 * tp + s
                        pe.wait_ge(y_taken, t + 1)
                        for k in range(K):
                            if k % (K // 2) == 0:
                                pe.wait_ge(hT_made, 2 * t + 2 * k // K + 3)
                            if k == K // 2:
                                turn(t + 1, 1 - s)
                            pe.wait_ge(wlo_made, k + 1)
                            for n in range(NY):
                                i = multiply(pe, y_ps[:, s], hT[:, s], whi, wlo, k, n)
                        i.then_inc(y_done, 1)

            @block.scalar
            def _(act):
                def take_h(t, s):
                    act.wait_ge(y_done, t + 1)
                    for n in range(2):
                        act.wait_ge(turned, 2 * t + n + 5)
                        act.activation(hT[:, s, 0, n * K // 2:(n + 1) * K // 2, :],
                                       hT_ps[:, n * K // 2:(n + 1) * K // 2, :], ACT.Copy, scale=X_SCALE
                                       ).then_inc(hi_made, 1)

                for n in range(2):
                    act.sem_inc(out_stored[n], 16)
                split_weights(None, act, None, w_out, stage, whi, wlo, w_loaded, whi_made, wlo_made)
                take_h(0, 0)
                with act.Fori(0, T // 2) as tp:
                    for s in range(2):
                        t = 2 * tp + s
                        take_h(t + 1, 1 - s)
                        act.wait_ge(low_made, t + 1)
                        act.activation(ex[:, s, :], low[:], ACT.Exp).then_inc(ex_made, 1)
                        act.wait_ge(res_made, t + 3)
                        act.dma_start(out[bass.ts(t, P), :], res[:, s, :]).then_inc(out_stored[s], 16)
                for n in range(2):
                    act.wait_ge(out_stored[n], 16 * (T // 2 + 1))

            @block.vector
            def _(dve):
                def take_lo(t, s):
                    for n in range(2):
                        ks = slice(n * K // 2, (n + 1) * K // 2)
                        dve.wait_ge(hi_made, 2 * t + n + 1)
                        dve.scalar_tensor_tensor(hT[:, s, 1, ks, :], hT_ps[:, ks, :], X_SCALE, hT[:, s, 0, ks, :],
                                                 ALU.mult, ALU.subtract).then_inc(hT_made, 1)

                dve.sem_inc(hT_made, 2)
                dve.sem_inc(y_taken, 2)
                dve.sem_inc(res_made, 2)
                split_weights(None, None, dve, w_out, stage, whi, wlo, w_loaded, whi_made, wlo_made)
                take_lo(0, 0)
                dve.wait_ge(bias_loaded, 16)
                with dve.Fori(0, T // 2) as tp:
                    for s in range(2):
                        t = 2 * tp + s
                        take_lo(t + 1, 1 - s)
                        dve.wait_ge(y_done, t + 3)
                        dve.scalar_tensor_tensor(y[:], y_ps[:, s, :], 1.0 / (X_SCALE * W_SCALE), bias[:],
                                                 ALU.mult, ALU.add).then_inc(y_taken, 1)
                        dve.wait_ge(y_taken, t + 3)
                        dve.tensor_scalar(low[:], y[:], 0.0, None, ALU.min).then_inc(low_made, 1)
                        dve.wait_ge(x_loaded[s], 16 * (tp + 1))
                        dve.wait_ge(res_made, t + 2)
                        dve.scalar_tensor_tensor(high[:], y[:], 0.0, x_in[:, s, :], ALU.max, ALU.add
                                                 ).then_inc(high_made, 1)
                        dve.wait_ge(ex_made, t + 1)
                        dve.wait_ge(high_made, t + 1)
                        dve.wait_ge(out_stored[s], 16 * (tp + 1))
                        dve.scalar_tensor_tensor(res[:, s, :], ex[:, s, :], -1.0, high[:], ALU.add, ALU.add
                                                 ).then_inc(res_made, 1)

    with ExitStack() as ctx:
        adjT = ctx.enter_context(nc.sbuf_tensor("adjT", [P, T, N], U8))
        with ExitStack() as inner:
            A = inner.enter_context(nc.sbuf_tensor("A", [P, T, H], F32))
            B = inner.enter_context(nc.sbuf_tensor("B", [P, T, H], F32))
            project(adjT, A, B)
            factors(A, B)
        attend(adjT)
    output()


_INS = ["x", "adj", "L0_gnn_W_seq", "L0_gnn_a1", "L0_gnn_a2", "L0_gnn_W_out", "L0_gnn_b_out"]


def kernel(**inputs):
    import numpy as _np
    import concourse.bacc as _bacc
    from concourse import mybir as _mybir
    from concourse.bass_utils import run_bass_kernel_spmd as _run

    nc = _bacc.Bacc("TRN2", target_bir_lowering=False, num_devices=1)
    arrays, args = {}, []
    for name in _INS:
        a = _np.ascontiguousarray(inputs[name])
        arrays[f"in_{name}"] = a
        args.append(nc.dram_tensor(f"in_{name}", a.shape, _mybir.dt.from_np(a.dtype), kind="ExternalInput").ap())
    out = nc.dram_tensor("out_0", inputs["x"].shape, _mybir.dt.float32, kind="ExternalOutput").ap()
    build(nc, *args, out)
    r = _run(nc, [arrays], core_ids=[0])
    return r.results[0]["out_0"]
```

```python
from contextlib import ExitStack

import concourse.bass as bass
from concourse import mybir

F32 = mybir.dt.float32
F16 = mybir.dt.float16
BF16 = mybir.dt.bfloat16
F8 = mybir.dt.float8e4
U8 = mybir.dt.uint8
I8 = mybir.dt.int8
U32 = mybir.dt.uint32
ALU = mybir.AluOpType
ACT = mybir.ActivationFunctionType
AX_X = mybir.AxisListType.X
RMAX = bass.bass_isa.ReduceOp.max

P = 128
ALPHA = 0.2
EPS = 1e-5
EDGE = 0xC0
TOP_BITS = 0x80808080
LO_SCALE = 4096.0
X_SCALE = 64.0
W_SCALE = 1024.0
E_SCALE = 64.0


def build(nc, x, adj, w_seq, a1, a2, w_out, b_out, out):
    N, D = x.shape
    DH = a1.shape[0]
    H = D // DH
    T = N // P
    K = D // P
    BANK = 512
    NY = D // BANK
    Q = 4
    QJ = T // Q

    IG = 8
    GI = IG * P
    NG = T // IG
    J = 4
    C = T // J
    M1_SLOTS, M0_SLOTS = 4, 2
    DC = DH + 1
    NV = 4 * DC
    QT = T // NG
    PK = 5 * T
    ON_DVE = (1, 1, 2, 1, 1, 1, 1, 1)
    assert T % IG == 0 and QT * NG == T and NV <= BANK

    seq_d = nc.dram_tensor("seq_by_head", (H, P, T, DH), F32, kind="Internal").ap()
    pack_d = nc.dram_tensor("pack_by_head", (H, P, PK), F32, kind="Internal").ap()
    arow_d = nc.dram_tensor("a_by_head", (H, N), F32, kind="Internal").ap()
    hid_d = nc.dram_tensor("hidden", (N, D), F32, kind="Internal").ap()

    def tools(ctx):
        return (lambda name, shape, dt: ctx.enter_context(nc.sbuf_tensor(name, shape, dt)),
                lambda name, shape, dt: ctx.enter_context(nc.psum_tensor(name, shape, dt)),
                lambda name: ctx.enter_context(nc.semaphore(name)))

    def split_weights(sp, act, dve, dram, stage, whi, wlo, loaded, hi_made, lo_made, k0=0, k1=K):
        slots = stage.shape[1]
        for k in range(k0, k1):
            s = k % slots
            if sp:
                if k >= slots:
                    sp.wait_ge(lo_made, k - slots + 1)
                sp.dma_start(stage[:, s, :], dram[k * P:(k + 1) * P, :]).then_inc(loaded[s], 16)
            if act:
                act.wait_ge(loaded[s], 16 * (k // slots + 1))
                act.activation(whi[:, k, :], stage[:, s, :], ACT.Copy, scale=W_SCALE).then_inc(hi_made, 1)
            if dve:
                dve.wait_ge(hi_made, k + 1)
                dve.scalar_tensor_tensor(wlo[:, k, :], stage[:, s, :], W_SCALE, whi[:, k, :], ALU.mult,
                                         ALU.subtract).then_inc(lo_made, 1)

    def multiply(pe, y, hT, whi, wlo, k, n):
        cols = slice(n * BANK, (n + 1) * BANK)
        pe.matmul(y[:, cols], hT[:, 0, k, :], whi[:, k, cols], start=k == 0, stop=False)
        pe.matmul(y[:, cols], hT[:, 0, k, :], wlo[:, k, cols], start=False, stop=False)
        return pe.matmul(y[:, cols], hT[:, 1, k, :], whi[:, k, cols], start=False, stop=k == K - 1)

    def identity(pool, tile, zeroed, made):
        pool.memset(tile, 0.0).then_inc(zeroed, 1)
        pool.wait_ge(zeroed, 1)
        pool.affine_select(out=tile, in_=tile, compare_op=ALU.not_equal, fill=1.0, base=0,
                           pattern=[[-1, P]], channel_multiplier=1).then_inc(made, 1)

    def project(adjT, A, B):
        with ExitStack() as ctx:
            sb, ps, sem = tools(ctx)
            whi = sb("w_seq_hi", [P, K, D], F16)
            wlo = sb("w_seq_lo", [P, K, D], F16)
            x_in = sb("x_in", [P, D], F32)
            xn = sb("xn", [P, D], F32)
            hT = sb("hT", [P, 2, 2, K, P], F16)
            seq = sb("seq", [P, H, DH], F32)
            prod = sb("prod", [P, H, DH], F32)
            adj_in = sb("adj_in", [P, Q, QJ * P], F32)
            ident = sb("ident", [P, P], F32)
            ident16 = sb("ident16", [P, P], BF16)
            a12 = sb("a12", [P, 2, DH], F32)
            stats = sb("stats", [P, 2, 6], F32)
            mv = sb("mv", [P, 2], F32)
            var = sb("var", [P, 1], F32)
            std = sb("std", [P, 1], F32)
            rstd = sb("rstd", [P, 1], F32)
            xT_ps = ps("xT_ps", [P, K, P], F32)
            y_ps = ps("y_ps", [P, 2, D], F32)
            adj_ps = ps("adj_ps", [P, 2, QJ, P], BF16)

            w_loaded = [sem(f"w_loaded{n}") for n in range(Q)]
            whi_made, wlo_made = sem("whi_made"), sem("wlo_made")
            hi_made = sem("hT_hi_made")
            a12_loaded = sem("a12_loaded")
            x_loaded = sem("x_loaded")
            adj_loaded = [sem(f"adj_loaded{q}") for q in range(Q)]
            adj_turned = sem("adj_turned")
            adj_bank_free = sem("adj_bank_free")
            zeroed, zeroed16 = sem("zeroed"), sem("zeroed16")
            ident_made = sem("ident_made")
            stats_made = sem("stats_made")
            stats_seen = sem("stats_seen")
            mv_made = sem("mv_made")
            var_made = sem("var_made")
            std_made = sem("std_made")
            rstd_made = sem("rstd_made")
            xn_made = sem("xn_made")
            xT_done = sem("xT_done")
            hT_made = sem("hT_made")
            y_done = sem("y_done")
            seq_made = sem("seq_made")
            seq_stored = sem("seq_stored")
            prod_made = sem("prod_made")
            score_made = sem("score_made")
            block = ctx.enter_context(nc.Block())

            @block.sync
            def _(sp):
                sp.dma_start(x_in[:], x[0:P, :]).then_inc(x_loaded, 16)
                sp.dma_start(a12[:, 0, :], a1.partition_broadcast(P)).then_inc(a12_loaded, 16)
                sp.dma_start(a12[:, 1, :], a2.partition_broadcast(P)).then_inc(a12_loaded, 16)
                split_weights(sp, None, None, w_seq, adj_in, whi, wlo, w_loaded, whi_made, wlo_made)
                sp.wait_ge(xn_made, 2)
                sp.dma_start(x_in[:], x[P:2 * P, :]).then_inc(x_loaded, 16)
                sp.wait_ge(wlo_made, K)
                with sp.Fori(0, T) as t:
                    for q in range(Q):
                        sp.wait_ge(adj_turned, Q * t + q + 1)
                        sp.dma_start(adj_in[:, q, :], adj[bass.ts(t, P), q * QJ * P:(q + 1) * QJ * P]
                                     ).then_inc(adj_loaded[q], 16)
                    sp.wait_ge(xn_made, t + 3)
                    sp.dma_start(x_in[:], x[bass.ts((t + 2) % T, P), :]).then_inc(x_loaded, 16)

            @block.gpsimd
            def _(pool):
                identity(pool, ident[:], zeroed, ident_made)
                identity(pool, ident16[:], zeroed16, ident_made)

            @block.vector
            def _(dve):
                def norm(t):
                    dve.wait_ge(x_loaded, 16 * (t + 1))
                    for n in range(2):
                        dve.bn_stats(stats[:, n, :], x_in[:, n * D // 2:(n + 1) * D // 2]).then_inc(stats_made, 1)
                    dve.wait_ge(stats_made, 2 * (t + 1))
                    dve.sem_inc(stats_seen, 1)
                    dve.wait_ge(xn_made, t + 1)
                    dve.sem_inc(stats_seen, 1)
                    dve.bn_aggr(mv[:], stats[:]).then_inc(mv_made, 1)
                    dve.wait_ge(mv_made, t + 1)
                    dve.tensor_scalar(var[:], mv[:, 1:2], EPS, None, ALU.add).then_inc(var_made, 1)
                    dve.wait_ge(std_made, t + 1)
                    dve.reciprocal(rstd[:], std[:]).then_inc(rstd_made, 1)
                    dve.wait_ge(rstd_made, t + 1)
                    dve.wait_ge(xT_done, 2 * t + 1)
                    dve.tensor_scalar(xn[:], x_in[:], mv[:, 0:1], rstd[:], ALU.subtract, ALU.mult
                                      ).then_inc(xn_made, 1)

                dve.sem_inc(seq_made, 2)
                dve.sem_inc(hT_made, 2)
                dve.sem_inc(xn_made, 1)
                dve.sem_inc(score_made, 1)
                def take_lo(t, s):
                    for n in range(2):
                        ks = slice(n * K // 2, (n + 1) * K // 2)
                        dve.wait_ge(hi_made, 2 * t + n + 1)
                        dve.scalar_tensor_tensor(hT[:, s, 1, ks, :], xT_ps[:, ks, :], 0.0, hT[:, s, 0, ks, :],
                                                 ALU.max, ALU.subtract).then_inc(hT_made, 1)

                norm(0)
                split_weights(None, None, dve, w_seq, adj_in, whi, wlo, w_loaded, whi_made, wlo_made)
                take_lo(0, 0)
                norm(1)
                dve.wait_ge(a12_loaded, 32)
                with dve.Fori(0, T // 2) as tp:
                    for s in range(2):
                        t = 2 * tp + s
                        take_lo(t + 1, 1 - s)
                        dve.wait_ge(y_done, t + 3)
                        dve.wait_ge(seq_stored, 16 * (t + 1))
                        dve.tensor_scalar(seq[:].rearrange("p h d -> p (h d)"), y_ps[:, s, :],
                                          1.0 / (X_SCALE * W_SCALE), None, ALU.mult).then_inc(seq_made, 1)
                        norm(t + 2)
                        dve.wait_ge(seq_made, t + 3)
                        for n, S in enumerate((A, B)):
                            dve.wait_ge(score_made, 2 * t + n + 1)
                            dve.tensor_tensor(prod[:], seq[:],
                                              a12[:, n:n + 1, :].to_broadcast([P, H, DH]), ALU.mult
                                              ).then_inc(prod_made, 1)
                            dve.wait_ge(prod_made, 2 * t + n + 1)
                            dve.tensor_reduce(S[:, bass.ds(t, 1), :], prod[:], AX_X, ALU.add
                                              ).then_inc(score_made, 1)

            @block.scalar
            def _(act):
                def root(t):
                    act.wait_ge(var_made, t + 1)
                    act.activation(std[:], var[:], ACT.Sqrt, scale=X_SCALE ** -2).then_inc(std_made, 1)

                def take_h(t, s):
                    act.wait_ge(y_done, t + 1)
                    for n in range(2):
                        act.wait_ge(xT_done, 2 * t + n + 2)
                        act.activation(hT[:, s, 0, n * K // 2:(n + 1) * K // 2, :],
                                       xT_ps[:, n * K // 2:(n + 1) * K // 2, :], ACT.Relu
                                       ).then_inc(hi_made, 1)

                def take_adj(t, q):
                    act.wait_ge(adj_turned, Q * (t + 1) + q + 1)
                    act.activation(adjT[:, q * QJ:(q + 1) * QJ, bass.ts(t, P)], adj_ps[:, q % 2, :, :],
                                   ACT.Copy, scale=float(EDGE)).then_inc(adj_bank_free, 1)

                act.sem_inc(adj_bank_free, 2)
                act.sem_inc(seq_stored, 16)
                root(0)
                split_weights(None, act, None, w_seq, adj_in, whi, wlo, w_loaded, whi_made, wlo_made)
                take_h(0, 0)
                root(1)
                with act.Fori(0, T // 2) as tp:
                    for s in range(2):
                        t = 2 * tp + s
                        take_h(t + 1, 1 - s)
                        for q in range(Q):
                            take_adj(t, q)
                        root(t + 2)
                        act.wait_ge(seq_made, t + 3)
                        act.dma_start(seq_d[:, :, bass.ds(t, 1), :].rearrange("h p t d -> p h (t d)"), seq[:]
                                      ).then_inc(seq_stored, 16)
                act.wait_ge(seq_stored, 16 * (T + 1))

            @block.tensor
            def _(pe):
                def turn_x(t):
                    pe.wait_ge(xn_made, t + 2)
                    pe.wait_ge(hT_made, 2 * t + 2)
                    for k in range(K):
                        i = pe.transpose(xT_ps[:, k, :], xn[:, k * P:(k + 1) * P], ident[:])
                        if k % (K // 2) == K // 2 - 1:
                            i.then_inc(xT_done, 1)

                def turn_adj(t, q):
                    pe.wait_ge(adj_loaded[q], 16 * (t + 1))
                    pe.wait_ge(adj_bank_free, Q * t + q + 1)
                    upper = adj_in[:, q, :].bitcast(BF16).rearrange("p (j c two) -> p j c two", j=QJ, two=2)
                    for j in range(QJ):
                        i = pe.transpose(adj_ps[:, q % 2, j, :], upper[:, j, :, 1], ident16[:])
                    i.then_inc(adj_turned, 1)

                pe.sem_inc(y_done, 2)
                pe.sem_inc(adj_turned, Q)
                pe.sem_inc(xT_done, 1)
                pe.wait_ge(ident_made, 2)
                turn_x(0)
                with pe.Fori(0, T // 2) as tp:
                    for s in range(2):
                        t = 2 * tp + s
                        pe.wait_ge(seq_made, t + 1)
                        for k in range(K):
                            if k % (K // 2) == 0:
                                pe.wait_ge(hT_made, 2 * t + 2 * k // K + 3)
                            if k == K // 2:
                                turn_x(t + 1)
                            if k >= K - Q:
                                turn_adj(t, k - K + Q)
                            pe.wait_ge(wlo_made, k + 1)
                            for n in range(NY):
                                i = multiply(pe, y_ps[:, s], hT[:, s], whi, wlo, k, n)
                        i.then_inc(y_done, 1)

    def attend(adjT, A, B, prod):
        with ExitStack() as ctx:
            sb, ps, sem = tools(ctx)
            arow = sb("arow", [P, 2, GI], F32)
            pack = sb("pack", [P, 2, PK], F32)
            seq1 = sb("seq1", [P, QT, DC], F32)
            m1 = sb("m1", [P, M1_SLOTS, J, GI], F8)
            m0 = sb("m0", [P, M0_SLOTS, J, GI], F8)
            vals_flat = sb("vals", [P, 2, T * NV], F16)
            vals = vals_flat[:].rearrange("p s (t m x d) -> p s t m x d", t=T, m=2, x=2)
            lo_part = sb("lo_part", [P, 2, 2, 2, DC], F32)
            side = sb("side", [P, IG, 2, DC], F32)
            both, hid = side[:, :, 0, :], side[:, :, 1, 0:DH]
            rden = sb("rden", [P, IG, 1], F32)
            acc = ps("acc", [P, IG, BANK], F32)

            aT = m1[:].rearrange("p s j i -> p (s j i)").bitcast(F32)[0:H, :]
            packs = vals_flat[:, 1, 0:2 * H * PK].bitcast(F32).rearrange("p (h c) -> p h c", h=H)
            args = m0[:].rearrange("p s j i -> p (s j i)").bitcast(F32).rearrange("p (x h t) -> p x h t", x=4, h=H)
            diff, z = args[:, 0], args[:, 1]
            zlo, zhi = args[:, 2], args[:, 3]
            ex2 = side[:].rearrange("p b m d -> p (b m d)")[:, 0:2 * H * T].rearrange(
                "p (x h t) -> p x h t", x=2, h=H)
            small = lo_part[:].rearrange("p a b x d -> p (a b x d)")
            ident_f, top, bmax = small[:, 0:P], small[:, P:P + H], small[:, P + H:P + 2 * H]
            aT_ps = acc[:, 0:2, :]

            ADJ_LOW_READ = 1 + C * (NG * H - 1) + C // 2

            def row(t, rows, dt):
                return adjT[:, t:t + rows, :].rearrange("p t n -> p (t n)").bitcast(dt)

            assert N == 4 * D and K == 8
            whi = row(0, 4, F16).rearrange("p (k d) -> p k d", k=K)
            wlo = row(4, 4, F16).rearrange("p (k d) -> p k d", k=K)
            h_in = row(8, 2, F32).rearrange("p (s d) -> p s d", s=2)
            x_in = row(10, 2, F32).rearrange("p (s d) -> p s d", s=2)
            hT = row(12, 2, F16).rearrange("p (s x k n) -> p s x k n", s=2, x=2, k=K)
            bias = row(14, 1, F32)
            y = row(16, 1, F32)
            low = row(17, 1, F32)
            ex = row(18, 2, F32).rearrange("p (s d) -> p s d", s=2)
            high = row(20, 1, F32)
            res = row(21, 2, F32).rearrange("p (s d) -> p s d", s=2)
            ident = row(23, 1, F32)[:, 0:P]
            stage = vals_flat[:, 0, 0:8 * D].bitcast(F32).rearrange("p (s d) -> p s d", s=4)
            hT_ps = acc[:, 0:2, :].rearrange("p b (k n) -> p (b k) n", n=P)
            y_ps = acc[:, 2:6, :].rearrange("p (s b) c -> p s (b c)", s=2)

            zeroed_f, ident_f_made = sem("zeroed_f"), sem("ident_f_made")
            top_made, bmax_made = sem("top_made"), sem("bmax_made")
            args_made, ex2_made = sem("args_made"), sem("ex2_made")
            packs_made = sem("packs_made")
            aT_done, aT_taken = sem("aT_done"), sem("aT_taken")
            arow_stored = [sem(f"arow_stored{n}") for n in range(2)]
            packs_stored = sem("packs_stored")

            arow_loaded = [sem(f"arow_loaded{n}") for n in range(2)]
            pack_loaded = [sem(f"pack_loaded{n}") for n in range(2)]
            seq_loaded = sem("seq_loaded")
            ones_made = sem("ones_made")
            prod_made = sem("prod_v_made")
            hi_made = sem("hi_made")
            vals_made = sem("vals_made")
            above_act = sem("above_act")
            above_dve = sem("above_dve")
            m1_made = sem("m1_made")
            m0_made = sem("m0_made")
            masks_used = sem("masks_used")
            waits_passed = sem("waits_passed")
            acc_done = sem("acc_done")
            lo_taken = sem("lo_taken")
            acc_free = sem("acc_free")
            sides_scaled = sem("sides_scaled")
            both_made = sem("both_made")
            rden_made = sem("rden_made")
            hid_made = sem("hid_made")
            hid_stored = sem("hid_stored")

            w_loaded = [sem(f"w_out_loaded{n}") for n in range(4)]
            whi_made, wlo_made = sem("w_out_hi_made"), sem("w_out_lo_made")
            hT_hi_made = sem("hT_hi_made_o")
            bias_loaded = sem("bias_loaded")
            h_loaded = [sem(f"h_loaded{n}") for n in range(2)]
            x_loaded = [sem(f"x_loaded_o{n}") for n in range(2)]
            zeroed, ident_made = sem("zeroed_o"), sem("ident_made_o")
            turned = sem("turned")
            hT_made = sem("hT_made_o")
            y_done = sem("y_done_o")
            y_taken = sem("y_taken")
            low_made, ex_made, high_made = sem("low_made"), sem("ex_made"), sem("high_made")
            res_made = sem("res_made")
            out_stored = [sem(f"out_stored{n}") for n in range(2)]
            block = ctx.enter_context(nc.Block())

            @block.sync
            def _(sp):
                def load_weights(k0, k1):
                    split_weights(sp, None, None, w_out, stage, whi, wlo, w_loaded, whi_made, wlo_made, k0, k1)

                def load_h(t, s):
                    sp.wait_ge(turned, 2 * t + 2)
                    sp.dma_start(h_in[:, s, :], hid_d[bass.ts(t % T, P), :]).then_inc(h_loaded[s], 16)

                def load_seq(h, q):
                    sp.dma_start(seq1[:, :, 0:DH], seq_d[bass.ds(h, 1), :, q * QT:(q + 1) * QT, :]
                                 .rearrange("h p t d -> (h p) t d")).then_inc(seq_loaded, 16)

                def load_pack(h, slot):
                    sp.dma_start(pack[:, slot, :], pack_d[bass.ds(h, 1), :, :].rearrange("h p c -> (h p) c")
                                 ).then_inc(pack_loaded[slot], 16)

                def load_arow(h, g, slot):
                    sp.dma_start(arow[:, slot, :], arow_d[bass.ds(h, 1), g * GI:(g + 1) * GI]
                                 .rearrange("h n -> (h n)").partition_broadcast(P)).then_inc(arow_loaded[slot], 16)

                sp.sem_inc(hid_stored, 16)
                load_seq(0, 0)
                sp.wait_ge(aT_taken, GI // BANK)
                sp.dma_start(arow_d[:, 0:GI], aT[:, 0:GI]).then_inc(arow_stored[0], 16)
                sp.wait_ge(arow_stored[0], 16)
                load_arow(0, 0, 0)
                sp.wait_ge(aT_taken, N // BANK)
                sp.dma_start(arow_d[:, GI:N], aT[:, GI:N]).then_inc(arow_stored[1], 16)
                sp.wait_ge(packs_made, 5)
                sp.dma_start(pack_d.rearrange("h p c -> p h c"), packs).then_inc(packs_stored, 16)

                for q in range(1, NG):
                    sp.wait_ge(prod_made, 2 * q)
                    load_seq(0, q)
                sp.wait_ge(prod_made, 2 * NG)
                load_seq(1, 0)
                sp.wait_ge(arow_stored[1], 16)
                sp.wait_ge(packs_stored, 16)

                def pair(hp, last):
                    for s in range(2):
                        for g in range(NG):
                            h = 2 * hp + s
                            n = h * NG + g
                            if g == 0 and not (last and s):
                                sp.wait_ge(sides_scaled, n + 1)
                                load_pack(h + 1, 1 - s)
                            if not (last and s and g == NG - 1):
                                sp.wait_ge(m1_made, C * n + 1)
                                load_arow(h + (g + 1) // NG, (g + 1) % NG, (g + 1) % 2)
                            if not (last and (s or g == NG - 1)):
                                sp.wait_ge(prod_made, 2 * (n + NG + 1))
                                load_seq(h + 1 + (g + 1) // NG, (g + 1) % NG)
                            if last and s and g == 0:
                                sp.wait_ge(masks_used, M1_SLOTS + C * NG * (H - 1))
                                load_weights(0, 4)
                            if last and s and g == NG - 1:
                                sp.wait_ge(m1_made, ADJ_LOW_READ)
                                load_weights(4, K)
                                sp.wait_ge(hid_stored, 16 * (n - NG + 2))
                                load_h(0, 0)
                                load_h(1, 1)
                                sp.dma_start(bias[:], b_out.partition_broadcast(P)).then_inc(bias_loaded, 16)
                            sp.wait_ge(hid_made, n + 2)
                            sp.dma_start(hid_d[g * GI:(g + 1) * GI, :]
                                         .rearrange("(t p) c -> p t c", p=P)[:, :, bass.ts(2 * hp + s, DH)],
                                         hid).then_inc(hid_stored, 16)

                with sp.Fori(0, H // 2 - 1) as hp:
                    pair(hp, False)
                pair(H // 2 - 1, True)
                sp.wait_ge(hid_stored, 16 * (H * NG + 1))
                with sp.Fori(0, T // 2) as tp:
                    for s in range(2):
                        t = 2 * tp + s
                        load_h(t + 2, s)
                        sp.wait_ge(res_made, t + 1)
                        sp.dma_start(x_in[:, s, :], x[bass.ts(t, P), :]).then_inc(x_loaded[s], 16)
                sp.wait_ge(h_loaded[1], 16 * (T // 2 + 1))

            @block.gpsimd
            def _(pool):
                identity(pool, ident_f, zeroed_f, ident_f_made)
                pool.wait_ge(top_made, 1)
                pool.partition_all_reduce(bmax, top, P, RMAX).then_inc(bmax_made, 1)
                pool.wait_ge(m1_made, 1 + C * NG * H)
                identity(pool, ident[:], zeroed, ident_made)

            @block.scalar
            def _(act):
                def compare(hp, s, g, c):
                    hs, gs = (s + (g // NG)) % 2, g % NG
                    grp = (2 * hp + s) * NG + g
                    n = grp * C + c
                    act.wait_ge(masks_used, n + 1)
                    if c == 0:
                        act.wait_ge(arow_loaded[gs % 2], 16 * ((2 * hp + s) * (NG // 2) + g // 2 + 1))
                    for j in range(J - ON_DVE[c]):
                        i = act.activation(m1[:, c % M1_SLOTS, j, :].bitcast(I8), arow[:, gs % 2, :], ACT.Sign,
                                           bias=pack[:, hs, c * J + j:c * J + j + 1], scale=-1.0)
                    i.then_inc(above_act, 1)

                def hi(q, slot, qq, e):
                    act.wait_ge(prod_made, 2 * q + e + 1)
                    act.activation(vals[:, slot, qq * QT:(qq + 1) * QT, e, 0, :], prod[:, e, :, :], ACT.Copy,
                                   scale=1.0 / LO_SCALE).then_inc(hi_made, 1)

                def split(k0, k1):
                    split_weights(None, act, None, w_out, stage, whi, wlo, w_loaded, whi_made, wlo_made, k0, k1)

                for g in range(N // BANK):
                    act.wait_ge(aT_done, g + 1)
                    act.activation(aT[:, g * BANK:(g + 1) * BANK], aT_ps[0:H, g % 2, :], ACT.Copy
                                   ).then_inc(aT_taken, 1)
                act.wait_ge(args_made, 4)
                act.activation(ex2[:, 0], diff, ACT.Exp).then_inc(ex2_made, 1)
                act.activation(ex2[:, 1], diff, ACT.Exp, scale=ALPHA).then_inc(ex2_made, 1)
                F = packs[:, :, 3 * T:5 * T].rearrange("p h (t two) -> p h t two", two=2)
                act.activation(F[:, :, :, 0], zlo, ACT.Exp).then_inc(packs_made, 1)
                act.activation(F[:, :, :, 1], zhi, ACT.Exp).then_inc(packs_made, 1)

                act.wait_ge(pack_loaded[0], 16)
                act.wait_ge(aT_taken, N // BANK)
                act.sem_inc(acc_free, 4)
                for q, chunks in enumerate(((0,), (1, 2), (3,), ())):
                    for e in range(2):
                        hi(q, 0, q, e)
                    for c in chunks:
                        compare(0, 0, 0, c)

                act.wait_ge(arow_stored[1], 16)
                act.wait_ge(packs_stored, 16)

                def pair(hp, last):
                    for s in range(2):
                        for g in range(NG):
                            n = (2 * hp + s) * NG + g
                            ending = last and s and g == NG - 1
                            for c in range(C // 2, C):
                                compare(hp, s, g, c)
                                if ending:
                                    if c == C // 2:
                                        act.wait_ge(m1_made, ADJ_LOW_READ)
                                    split(c - C // 2, c - C // 2 + 1)
                                if c in (C // 2 + 1, C // 2 + 2) and not (last and s):
                                    if g == 0 and c == C // 2 + 1:
                                        act.wait_ge(masks_used, M1_SLOTS + C * n)
                                    hi(n + NG, 1 - s, g, c - C // 2 - 1)
                            if ending:
                                split(C // 2, K)
                            elif g == NG - 1:
                                act.wait_ge(pack_loaded[1 - s], 16 * (hp + 1 + s))
                            for c in range(0 if ending else C // 2 - 1):
                                compare(hp, s, g + 1, c)
                            for p in range(IG // 2):
                                if p < IG // 2 - 1:
                                    act.wait_ge(acc_done, 3 * n + p + 1)
                                else:
                                    act.wait_ge(masks_used, M1_SLOTS + C * (n + 1))
                                act.wait_ge(acc_free, 4 * n + p + 3)
                                acc4 = acc[:, 2 * p:2 * p + 2, 0:NV].rearrange("p b (m x d) -> p b m x d", m=2, x=2)
                                act.activation(lo_part[:, p % 2], acc4[:, :, :, 1, :], ACT.Copy,
                                               scale=1.0 / LO_SCALE).then_inc(lo_taken, 1)
                            if not ending:
                                compare(hp, s, g + 1, C // 2 - 1)

                with act.Fori(0, H // 2 - 1) as hp:
                    pair(hp, False)
                pair(H // 2 - 1, True)

                def take_h(t, s):
                    act.wait_ge(y_done, t + 1)
                    for n in range(2):
                        act.wait_ge(turned, 2 * t + n + 5)
                        act.activation(hT[:, s, 0, n * K // 2:(n + 1) * K // 2, :],
                                       hT_ps[:, n * K // 2:(n + 1) * K // 2, :], ACT.Copy, scale=X_SCALE
                                       ).then_inc(hT_hi_made, 1)

                for n in range(2):
                    act.sem_inc(out_stored[n], 16)
                take_h(0, 0)
                with act.Fori(0, T // 2) as tp:
                    for s in range(2):
                        t = 2 * tp + s
                        take_h(t + 1, 1 - s)
                        act.wait_ge(low_made, t + 1)
                        act.activation(ex[:, s, :], low[:], ACT.Exp).then_inc(ex_made, 1)
                        act.wait_ge(res_made, t + 3)
                        act.dma_start(out[bass.ts(t, P), :], res[:, s, :]).then_inc(out_stored[s], 16)
                for n in range(2):
                    act.wait_ge(out_stored[n], 16 * (T // 2 + 1))

            @block.vector
            def _(dve):
                def split(k0, k1):
                    split_weights(None, None, dve, w_out, stage, whi, wlo, w_loaded, whi_made, wlo_made, k0, k1)

                def take_lo(t, s):
                    for n in range(2):
                        ks = slice(n * K // 2, (n + 1) * K // 2)
                        dve.wait_ge(hT_hi_made, 2 * t + n + 1)
                        dve.scalar_tensor_tensor(hT[:, s, 1, ks, :], hT_ps[:, ks, :], X_SCALE, hT[:, s, 0, ks, :],
                                                 ALU.mult, ALU.subtract).then_inc(hT_made, 1)

                def compare(hp, s, g, c):
                    hs, gs = (s + (g // NG)) % 2, g % NG
                    n = ((2 * hp + s) * NG + g) * C + c
                    dve.wait_ge(masks_used, n + 1)
                    dve.wait_ge(arow_loaded[gs % 2], 16 * ((2 * hp + s) * (NG // 2) + g // 2 + 1))
                    for j in range(J - ON_DVE[c], J):
                        i = dve.tensor_scalar(m1[:, c % M1_SLOTS, j, :].bitcast(U8), arow[:, gs % 2, :],
                                              pack[:, hs, c * J + j:c * J + j + 1], 255.0, ALU.is_gt, ALU.mult)
                    i.then_inc(above_dve, 1)

                def adj_bits(g, c):
                    return adjT[:, c * J:(c + 1) * J, (g % NG) * GI:(g % NG + 1) * GI].bitcast(U32)

                def mask1(hp, s, g, c, between=None, final=False):
                    n = ((2 * hp + s) * NG + g) * C + c
                    dve.wait_ge(above_dve, n + 1)
                    dve.wait_ge(above_act, n + 1)
                    m = m1[:, c % M1_SLOTS].bitcast(U32)
                    dve.scalar_tensor_tensor(m, m, TOP_BITS, adj_bits(g, c), ALU.bitwise_xor, ALU.bitwise_and
                                             ).then_inc(m1_made, 1)
                    if between:
                        between()
                    if not final:
                        compare(hp, s, g + (c + 1) // C, (c + 1) % C)

                def mask0(hp, s, g, c):
                    n = ((2 * hp + s) * NG + g) * C + c
                    dve.wait_ge(m1_made, n + 2)
                    dve.wait_ge(masks_used, n + 1 + M1_SLOTS - M0_SLOTS)
                    dve.tensor_scalar(m0[:, c % M0_SLOTS].bitcast(U32), m1[:, c % M1_SLOTS].bitcast(U32),
                                      TOP_BITS, 1, ALU.bitwise_and, ALU.logical_shift_right).then_inc(m0_made, 1)

                def prepare(q, slot, qq, e):
                    E = pack[:, slot, (e + 1) * T + qq * QT:(e + 1) * T + (qq + 1) * QT]
                    dve.wait_ge(seq_loaded, 16 * (q + 1))
                    if not isinstance(q, int) or q:
                        dve.wait_ge(vals_made, 2 * q + e - 1)
                    dve.tensor_tensor(prod[:, e], seq1[:], E.unsqueeze(2).to_broadcast([P, QT, DC]), ALU.mult
                                      ).then_inc(prod_made, 1)

                def lo(q, slot, qq, e):
                    v = vals[:, slot, qq * QT:(qq + 1) * QT, e]
                    dve.wait_ge(prod_made, 2 * q + e + 1)
                    dve.wait_ge(hi_made, 2 * q + e + 1)
                    dve.scalar_tensor_tensor(v[:, :, 1, :], v[:, :, 0, :], -LO_SCALE, prod[:, e], ALU.mult, ALU.add
                                             ).then_inc(vals_made, 1)

                def take(n, p):
                    acc4 = acc[:, 2 * p:2 * p + 2, 0:NV].rearrange("p b (m x d) -> p b m x d", m=2, x=2)
                    dve.wait_ge(lo_taken, 4 * n + p + 1)
                    dve.tensor_tensor(side[:, 2 * p:2 * p + 2], lo_part[:, p % 2], acc4[:, :, :, 0, :], ALU.add
                                      ).then_inc(acc_free, 1)

                dve.sem_inc(m1_made, 1)
                dve.sem_inc(sides_scaled, 1)
                dve.sem_inc(hid_made, 1)
                dve.sem_inc(hT_made, 2)
                dve.sem_inc(y_taken, 2)
                dve.sem_inc(res_made, 2)
                def heads_first(S):
                    return S.rearrange("p t h -> p h t")

                dve.tensor_reduce(top, heads_first(B), AX_X, ALU.max).then_inc(top_made, 1)
                dve.tensor_scalar(packs[:, :, 0:T], heads_first(B), -1.0, None, ALU.mult).then_inc(packs_made, 1)
                dve.memset(seq1[:, :, DH:DC], 1.0).then_inc(ones_made, 1)
                dve.wait_ge(bmax_made, 1)
                wide = bmax.unsqueeze(2).to_broadcast([P, H, T])
                dve.tensor_tensor(diff, heads_first(B), wide, ALU.subtract).then_inc(args_made, 1)
                dve.tensor_tensor(z, heads_first(A), wide, ALU.add).then_inc(args_made, 1)
                dve.wait_ge(args_made, 2)
                dve.tensor_scalar(zlo, z, 0.0, 1.0 - ALPHA, ALU.min, ALU.mult).then_inc(args_made, 1)
                dve.tensor_scalar(zhi, z, 0.0, ALPHA - 1.0, ALU.max, ALU.mult).then_inc(args_made, 1)
                dve.wait_ge(ex2_made, 2)
                for n in range(2):
                    dve.tensor_scalar(packs[:, :, (n + 1) * T:(n + 2) * T], ex2[:, n], E_SCALE * LO_SCALE,
                                      None, ALU.mult).then_inc(packs_made, 1)
                dve.wait_ge(packs_made, 5)
                dve.tensor_scalar(pack[:, 0, :], packs[:, 0, :], 1.0, None, ALU.mult).then_inc(pack_loaded[0], 16)

                dve.wait_ge(ones_made, 1)
                dve.wait_ge(pack_loaded[0], 16)
                dve.wait_ge(aT_done, N // BANK)

                def prepare_first(q):
                    for e in range(2):
                        prepare(q, 0, q, e)

                def lo_first(q):
                    for e in range(2):
                        lo(q, 0, q, e)

                prepare_first(0)
                lo_first(0)
                compare(0, 0, 0, 0)
                for c, between in enumerate((lambda: prepare_first(1), lambda: lo_first(1),
                                             lambda: prepare_first(2), lambda: lo_first(2))):
                    mask1(0, 0, 0, c, between)
                    mask0(0, 0, 0, c)
                prepare_first(3)
                lo_first(3)

                def pair(hp, last):
                    for s in range(2):
                        for g in range(NG):
                            n = (2 * hp + s) * NG + g
                            ending = last and s and g == NG - 1

                            def take_all():
                                dve.wait_ge(hid_stored, 16 * (n + 1))
                                for p in range(IG // 2):
                                    take(n, p)

                            def scale():
                                F = pack[:, s, 3 * T + 2 * IG * g:3 * T + 2 * IG * (g + 1)]
                                side_m = side[:].rearrange("p b m d -> p (b m) d")
                                dve.wait_ge(acc_free, 4 * n + 8)
                                dve.tensor_tensor(side_m, side_m, F.unsqueeze(2).to_broadcast([P, 2 * IG, DC]),
                                                  ALU.mult).then_inc(sides_scaled, 1)

                            def add():
                                dve.wait_ge(sides_scaled, n + 2)
                                dve.tensor_tensor(both, side[:, :, 0, :], side[:, :, 1, :], ALU.add
                                                  ).then_inc(both_made, 1)

                            def invert():
                                dve.wait_ge(both_made, n + 1)
                                dve.reciprocal(rden[:], both[:, :, DH:DC]).then_inc(rden_made, 1)

                            def divide():
                                dve.wait_ge(rden_made, n + 1)
                                dve.tensor_tensor(hid, both[:, :, 0:DH], rden[:].to_broadcast([P, IG, DH]),
                                                  ALU.mult).then_inc(hid_made, 1)

                            if g == 0 and not (last and s):
                                dve.wait_ge(pack_loaded[1 - s], 16 * (hp + 1 + s))
                            q = n + NG
                            ahead = (lambda: prepare(q, 1 - s, g, 0), lambda: prepare(q, 1 - s, g, 1),
                                     lambda: lo(q, 1 - s, g, 0), lambda: lo(q, 1 - s, g, 1))
                            if last and s:
                                ahead = [None] * 4
                            if ending:
                                ahead = [lambda k=k: split(k, k + 1) for k in range(4)]
                                dve.wait_ge(m1_made, ADJ_LOW_READ)
                            for k in range(C // 2):
                                mask1(hp, s, g, C // 2 + k, ahead[k], ending and k == C // 2 - 1)
                                mask0(hp, s, g, C // 2 + k)
                            if ending:
                                split(4, K)
                                take_all()
                                take_lo(0, 0)
                                scale()
                                add()
                                invert()
                                divide()
                                continue
                            mask1(hp, s, g + 1, 0)
                            mask0(hp, s, g + 1, 0)
                            mask1(hp, s, g + 1, 1, take_all)
                            mask0(hp, s, g + 1, 1)
                            scale()
                            mask1(hp, s, g + 1, 2, add)
                            mask0(hp, s, g + 1, 2)
                            invert()
                            mask1(hp, s, g + 1, 3, divide)
                            mask0(hp, s, g + 1, 3)

                with dve.Fori(0, H // 2 - 1) as hp:
                    pair(hp, False)
                pair(H // 2 - 1, True)
                dve.wait_ge(m1_made, 1 + C * NG * H)
                dve.wait_ge(bias_loaded, 16)
                with dve.Fori(0, T // 2) as tp:
                    for s in range(2):
                        t = 2 * tp + s
                        take_lo(t + 1, 1 - s)
                        dve.wait_ge(y_done, t + 3)
                        dve.scalar_tensor_tensor(y[:], y_ps[:, s, :], 1.0 / (X_SCALE * W_SCALE), bias[:],
                                                 ALU.mult, ALU.add).then_inc(y_taken, 1)
                        dve.wait_ge(y_taken, t + 3)
                        dve.tensor_scalar(low[:], y[:], 0.0, None, ALU.min).then_inc(low_made, 1)
                        dve.wait_ge(x_loaded[s], 16 * (tp + 1))
                        dve.wait_ge(res_made, t + 2)
                        dve.scalar_tensor_tensor(high[:], y[:], 0.0, x_in[:, s, :], ALU.max, ALU.add
                                                 ).then_inc(high_made, 1)
                        dve.wait_ge(ex_made, t + 1)
                        dve.wait_ge(high_made, t + 1)
                        dve.wait_ge(out_stored[s], 16 * (tp + 1))
                        dve.scalar_tensor_tensor(res[:, s, :], ex[:, s, :], -1.0, high[:], ALU.add, ALU.add
                                                 ).then_inc(res_made, 1)

            @block.tensor
            def _(pe):
                def turn(t, s):
                    pe.wait_ge(h_loaded[s], 16 * (t // 2 + 1))
                    pe.wait_ge(hT_made, 2 * t + 2)
                    for k in range(K):
                        i = pe.transpose(hT_ps[:, k, :], h_in[:, s, k * P:(k + 1) * P], ident[:])
                        if k % (K // 2) == K // 2 - 1:
                            i.then_inc(turned, 1)

                pe.wait_ge(ident_f_made, 1)
                for g in range(N // BANK):
                    if g >= 2:
                        pe.wait_ge(aT_taken, g - 1)
                    for n in range(BANK // P):
                        i = pe.transpose(aT_ps[0:H, g % 2, n * P:(n + 1) * P], A[:, g * BANK // P + n, :], ident_f)
                    i.then_inc(aT_done, 1)

                pe.sem_inc(masks_used, M1_SLOTS)
                pe.sem_inc(turned, 4)
                pe.sem_inc(y_done, 2)
                with pe.Fori(0, H // 2) as hp:
                    for s in range(2):
                        with pe.Fori(0, NG) as g:
                            n = (2 * hp + s) * NG + g
                            for c in range(C):
                                if c % 2 == 0:
                                    pe.wait_ge(vals_made, 2 * (NG * (2 * hp + s) + c // 2 + 1))
                                pe.wait_ge(m0_made, C * n + c + 1)
                                pe.sem_inc(waits_passed, 1)
                                for t in range(IG):
                                    if c == 0 and t % 2 == 0:
                                        pe.wait_ge(acc_free, 4 * n + t // 2 + 1)
                                        pe.sem_inc(waits_passed, 1)
                                    for j in range(J):
                                        v = vals[:, s, c * J + j].rearrange("p m x d -> p m (x d)")
                                        first, last = c == 0 and j == 0, c == C - 1 and j == J - 1
                                        for m, mask in enumerate((m1, m0)):
                                            slot = c % (M0_SLOTS if m else M1_SLOTS)
                                            i = pe.matmul(acc[:, t, m * 2 * DC:(m + 1) * 2 * DC],
                                                          mask[:, slot, j, t * P:(t + 1) * P], v[:, m, :],
                                                          start=first and m == 0, stop=last and m == 1,
                                                          skip_group_check=True)
                                    if c == C - 1 and t % 2 == 1 and t < IG - 1:
                                        i.then_inc(acc_done, 1)
                                i.then_inc(masks_used, 1)
                pe.wait_ge(ident_made, 1)
                pe.wait_ge(acc_free, 4 * NG * H + 1)
                turn(0, 0)
                pe.wait_ge(acc_free, 4 * NG * H + 3)
                with pe.Fori(0, T // 2) as tp:
                    for s in range(2):
                        t = 2 * tp + s
                        pe.wait_ge(y_taken, t + 1)
                        for k in range(K):
                            if k % (K // 2) == 0:
                                pe.wait_ge(hT_made, 2 * t + 2 * k // K + 3)
                            if k == K // 2:
                                turn(t + 1, 1 - s)
                            pe.wait_ge(wlo_made, k + 1)
                            for n in range(NY):
                                i = multiply(pe, y_ps[:, s], hT[:, s], whi, wlo, k, n)
                        i.then_inc(y_done, 1)

    with ExitStack() as ctx:
        adjT = ctx.enter_context(nc.sbuf_tensor("adjT", [P, T, N], U8))
        scores = ctx.enter_context(nc.sbuf_tensor("scores", [P, max(2 * T * H, 2 * QT * DC)], F32))
        A, B = (scores[:, n * T * H:(n + 1) * T * H].rearrange("p (t h) -> p t h", t=T) for n in range(2))
        prod = scores[:, 0:2 * QT * DC].rearrange("p (e t d) -> p e t d", e=2, t=QT)
        project(adjT, A, B)
        attend(adjT, A, B, prod)


_INS = ["x", "adj", "L0_gnn_W_seq", "L0_gnn_a1", "L0_gnn_a2", "L0_gnn_W_out", "L0_gnn_b_out"]


def kernel(**inputs):
    import numpy as _np
    import concourse.bacc as _bacc
    from concourse import mybir as _mybir
    from concourse.bass_utils import run_bass_kernel_spmd as _run

    nc = _bacc.Bacc("TRN2", target_bir_lowering=False, num_devices=1)
    arrays, args = {}, []
    for name in _INS:
        a = _np.ascontiguousarray(inputs[name])
        arrays[f"in_{name}"] = a
        args.append(nc.dram_tensor(f"in_{name}", a.shape, _mybir.dt.from_np(a.dtype), kind="ExternalInput").ap())
    out = nc.dram_tensor("out_0", inputs["x"].shape, _mybir.dt.float32, kind="ExternalOutput").ap()
    build(nc, *args, out)
    r = _run(nc, [arrays], core_ids=[0])
    return r.results[0]["out_0"]
```
